# Optimizing a Trainium2 kernel written in Bass

```python
import numpy as np
import jax
import jax.numpy as jnp

def _softmax(x, axis=-1):
    return jax.nn.softmax(x, axis=axis)

def _gelu(x):
    return jax.nn.gelu(x, approximate=True)

def _silu(x):
    return jax.nn.silu(x)

def _sigmoid(x):
    return jax.nn.sigmoid(x)

def _layernorm(x, axis=-1, eps=1e-05):
    m = jnp.mean(x, axis=axis, keepdims=True)
    v = jnp.var(x, axis=axis, keepdims=True)
    return (x - m) / jnp.sqrt(v + eps)

def _scatter_add(tgt, idx, src, axis=0):
    return tgt.at[idx].add(src)

def _segment_sum(src, seg, n):
    return jax.ops.segment_sum(src, seg, n)
kernel_name = 'mk_gnn_ffn_d1_gnn_r32_f8c9f7'

def setup_inputs(seed: int=0):
    np.random.seed(seed)
    _w = jnp.asarray

    def _rec_inputs():
        import jax
        import jax.numpy as jnp
        _gk = jax.random.key(seed)
        x = -0.0002117 + 1 * jax.random.normal(jax.random.fold_in(_gk, 1), (3125, 256), jnp.float32)
        src = jax.random.randint(jax.random.fold_in(_gk, 2), (50000,), 0, 3125, jnp.int32)
        dst = jax.random.randint(jax.random.fold_in(_gk, 3), (50000,), 0, 3125, jnp.int32)
        _o = jnp.argsort(dst, stable=True)
        src = src[_o]
        dst = dst[_o]
        edge_weight = jax.random.uniform(jax.random.fold_in(_gk, 12), (50000,), jnp.float32, 0.0, 1)
        return (x, src, dst, edge_weight)
    x, src, dst, edge_weight = _rec_inputs()

    def _L0_gnn_setup():
        import jax, jax.numpy as jnp
        import numpy as np
        N_NODES = 3125
        N_EDGES = 50000
        D_IN = 256
        D_OUT = 256
        key = jax.random.key(seed)
        k1, k2, k3, k4, k5 = jax.random.split(key, 5)
        x = jax.random.normal(k1, (N_NODES, D_IN), dtype=jnp.float32)
        edge_src = jax.random.randint(k2, (N_EDGES,), 0, N_NODES, dtype=jnp.int32)
        edge_dst = jax.random.randint(k3, (N_EDGES,), 0, N_NODES, dtype=jnp.int32)
        edge_val = jax.random.uniform(k4, (N_EDGES,), dtype=jnp.float32)
        stdv = 1.0 / np.sqrt(D_OUT)
        weight = jax.random.uniform(k5, (D_IN, D_OUT), dtype=jnp.float32, minval=-stdv, maxval=stdv)
        return {'x': x, 'edge_src': edge_src, 'edge_dst': edge_dst, 'edge_val': edge_val, 'weight': weight}
    _L0_gnn_all = _L0_gnn_setup()
    _L0_gnn_in = {k: v for k, v in _L0_gnn_all.items() if k in ('weight',)}
    del _L0_gnn_all

    def _L0_ffn_setup():
        import math
        import jax, jax.numpy as jnp
        import numpy as np
        CAPACITY_FACTOR = 1.25
        TOP_K = 2
        LN_EPS = 1e-05

        def _layer_norm(x, gamma, beta):
            mu = jnp.mean(x, axis=-1, keepdims=True)
            var = jnp.var(x, axis=-1, keepdims=True)
            return (x - mu) * jax.lax.rsqrt(var + LN_EPS) * gamma + beta
        key = jax.random.key(seed)
        ks = jax.random.split(key, 4)
        B, S, D, F, E = (8, 128, 256, 512, 8)
        x = jax.random.normal(ks[0], (B, S, D), dtype=jnp.float32)
        Wr = jax.random.normal(ks[1], (D, E), dtype=jnp.float32) / np.sqrt(D)
        br = jnp.zeros((E,), jnp.float32)
        W1 = jax.random.normal(ks[2], (E, D, F), dtype=jnp.float32) / np.sqrt(D)
        b1 = jnp.zeros((E, F), jnp.float32)
        W2 = jax.random.normal(ks[3], (E, F, D), dtype=jnp.float32) / np.sqrt(F)
        b2 = jnp.zeros((E, D), jnp.float32)
        gamma = jnp.ones((D,), jnp.float32)
        beta = jnp.zeros((D,), jnp.float32)
        return {'x': x, 'Wr': Wr, 'br': br, 'W1': W1, 'b1': b1, 'W2': W2, 'b2': b2, 'gamma': gamma, 'beta': beta}
    _L0_ffn_all = _L0_ffn_setup()
    _L0_ffn_in = {k: v for k, v in _L0_ffn_all.items() if k in ('Wr', 'br', 'W1', 'b1', 'W2', 'b2', 'gamma', 'beta')}
    del _L0_ffn_all
    return {'x': x, 'src': src, 'dst': dst, 'edge_weight': edge_weight, 'L0_gnn_weight': _L0_gnn_in['weight'], 'L0_ffn_Wr': _L0_ffn_in['Wr'], 'L0_ffn_br': _L0_ffn_in['br'], 'L0_ffn_W1': _L0_ffn_in['W1'], 'L0_ffn_b1': _L0_ffn_in['b1'], 'L0_ffn_W2': _L0_ffn_in['W2'], 'L0_ffn_b2': _L0_ffn_in['b2'], 'L0_ffn_gamma': _L0_ffn_in['gamma'], 'L0_ffn_beta': _L0_ffn_in['beta']}

def reference(x, src, dst, edge_weight, L0_gnn_weight, L0_ffn_Wr, L0_ffn_br, L0_ffn_W1, L0_ffn_b1, L0_ffn_W2, L0_ffn_b2, L0_ffn_gamma, L0_ffn_beta):
    import jax
    import jax.numpy as jnp

    def _L0_gnn_ref(x, edge_src, edge_dst, edge_val, weight):
        import jax, jax.numpy as jnp
        import numpy as np
        N_NODES = 3125
        N_EDGES = 50000
        D_IN = 256
        D_OUT = 256
        msgs = x[edge_src] * edge_val[:, None]
        agg = jax.ops.segment_sum(msgs, edge_dst, num_segments=x.shape[0])
        return agg @ weight

    def _L0_ffn_ref(x, Wr, br, W1, b1, W2, b2, gamma, beta):
        import math
        import jax, jax.numpy as jnp
        import numpy as np
        CAPACITY_FACTOR = 1.25
        TOP_K = 2
        LN_EPS = 1e-05

        def _layer_norm(x, gamma, beta):
            mu = jnp.mean(x, axis=-1, keepdims=True)
            var = jnp.var(x, axis=-1, keepdims=True)
            return (x - mu) * jax.lax.rsqrt(var + LN_EPS) * gamma + beta
        B, S, D = x.shape
        E = Wr.shape[1]
        N = B * S
        K = TOP_K
        logits = jnp.mean(x, axis=1) @ Wr + br
        routing_weights = jax.nn.softmax(logits, axis=-1)
        capacity = float(math.ceil(N * CAPACITY_FACTOR / E))
        expected_loads = routing_weights.sum(axis=0) * (N / B)
        scale = jnp.where(expected_loads > capacity, capacity / expected_loads, 1.0)
        routing_weights = jax.nn.softmax(routing_weights * scale, axis=-1)
        rw_tok = jnp.broadcast_to(routing_weights[:, None, :], (B, S, E)).reshape(N, E)
        top_w, top_i = jax.lax.top_k(rw_tok, K)
        top_w = jax.nn.softmax(top_w, axis=-1)
        xf = x.reshape(N, D)
        h = jax.nn.gelu(jnp.einsum('nd,edf->enf', xf, W1) + b1[:, None, :], approximate=False)
        y = jnp.einsum('enf,efd->end', h, W2) + b2[:, None, :]
        w_dense = jnp.zeros((N, E), x.dtype).at[jnp.arange(N)[:, None], top_i].add(top_w)
        out = jnp.einsum('ne,end->nd', w_dense, y).reshape(B, S, D)
        out = _layer_norm(out + x, gamma, beta)
        return out
    x = x + _L0_gnn_ref(_layernorm(x, axis=-1), src, dst, edge_weight, L0_gnn_weight)
    x = x + _L0_ffn_ref(_layernorm(x, axis=-1)[None], L0_ffn_Wr, L0_ffn_br, L0_ffn_W1, L0_ffn_b1, L0_ffn_W2, L0_ffn_b2, L0_ffn_gamma, L0_ffn_beta)[0]
    return x

_drawn_inputs = setup_inputs


def setup_inputs(seed=0):
    import zlib

    import numpy as np

    out = dict(_drawn_inputs(seed))
    spreads = {'L0_ffn_br': (0.0, 0.1),
     'L0_ffn_b1': (0.0, 0.491),
     'L0_ffn_b2': (0.0, 0.332),
     'L0_ffn_gamma': (1.0, 0.2),
     'L0_ffn_beta': (0.0, 0.1)}
    factors = {'L0_ffn_Wr': 8.0}
    for name, (base, spread) in spreads.items():
        noise = np.random.default_rng([zlib.crc32(name.encode()), seed]).standard_normal(out[name].shape)
        drawn = base * np.exp(spread * noise) if base else spread * noise
        out[name] = jnp.asarray(drawn.astype(out[name].dtype))
    for name, factor in factors.items():
        out[name] = (out[name] * factor).astype(out[name].dtype)
    return out
```

```python
import math
from contextlib import ExitStack

import concourse.bass as bass
from concourse import mybir

ALU = mybir.AluOpType
ACT = mybir.ActivationFunctionType
AX = mybir.AxisListType
F32 = mybir.dt.float32
I32 = mybir.dt.int32
U32 = mybir.dt.uint32

P = 128
EPS = 1e-5
CHUNKS = 4
GROUP = CHUNKS * P
WIN = 64
SLOTS = 7
SUM_BANKS = 4
SUM_GAP = 3
LAG = 3
TILE_SLOTS = 5
CAPACITY_FACTOR = 1.25

PREP_SRC, PREP_REL, PREP_FLAG, PREP_ALL = 1, 5, 10, 13
ROUTE_COLS, ROUTE_MAX0, ROUTE_MAX1, ROUTE_TOP, ROUTE_DENSE, ROUTE_BIAS = 2, 5, 16, 21, 27, 30
PICKED = 2
ROOT_MAGIC = float(0x5F3759DF)
NEWTON = 3
NEWTON_STEPS = 3 + 3 * NEWTON


def gnn_moe(nc, x, src, dst, edge_weight, gnn_w, wr, br, w1, b1, w2, b2, gamma, beta, out):
    nodes, dim = x.shape
    edges = src.shape[0]
    experts, _, hidden = w1.shape
    KD = dim // P
    FB = hidden // P
    groups = -(-edges // GROUP)
    full = edges // GROUP
    rest = edges - full * GROUP
    even = full // 16 * 16
    rounds = groups // SLOTS
    assert groups == rounds * SLOTS and groups == full + 1 and groups <= P
    tiles = -(-nodes // P)
    tail = nodes - (tiles - 1) * P
    width = tiles * P
    assert tiles % TILE_SLOTS == 0 and nodes - 1 + WIN <= width
    tile_rounds = tiles // TILE_SLOTS
    windows = width // WIN
    SPAN = 4 * P
    spans = (tiles - 1) // 4
    assert spans * 4 + 1 == tiles and spans % 2 == 0 and tail <= 64
    TAILW = 64
    capacity = float(math.ceil(nodes * CAPACITY_FACTOR / experts))

    with ExitStack() as ctx:
        def sb(name, shape, dt=F32):
            return ctx.enter_context(nc.sbuf_tensor(name, shape, dt))

        def sem(name):
            return ctx.enter_context(nc.semaphore(name))

        src_rows = sb("src_rows", [P, GROUP], I32)
        dst_rows = sb("dst_rows", [P, GROUP], I32)
        wgt_rows = sb("wgt_rows", [P, GROUP])
        src_f = sb("src_f", [P, GROUP])
        dst_f = sb("dst_f", [P, GROUP])
        rel_f = sb("rel_f", [P, GROUP])
        g_min = sb("g_min", [P, 1])
        g_max = sb("g_max", [P, 1])
        base_i = sb("base_i", [1, P], I32)
        span_row = sb("span_row", [1, P])
        span_max = sb("span_max", [1, 1])
        behind = sb("behind", [1, 1], I32)
        idx_t = sb("idx_t", [P, groups + SLOTS, CHUNKS], I32)
        rel_t = sb("rel_t", [P, groups, CHUNKS])
        wgt_t = sb("wgt_t", [P, groups, CHUNKS])
        dst_t = sb("dst_t", [P, groups, CHUNKS])
        idx_slot = sb("idx_slot", [P, SLOTS, CHUNKS], I32)
        ring = sb("ring", [P, 2 * SLOTS * CHUNKS * dim])
        half = SLOTS * CHUNKS * dim
        raw = ring[:, 0:half].rearrange("p (s c d) -> p s c d", s=SLOTS, c=CHUNKS)
        xn = ring[:, half:2 * half].rearrange("p (s c d) -> p s c d", s=SLOTS, c=CHUNKS)
        onehot = sb("onehot", [P, SLOTS, CHUNKS, WIN])
        bstats = sb("bstats", [P, SLOTS, CHUNKS, 6])
        meanvar = sb("meanvar", [P, SLOTS, CHUNKS, 2])
        dev = sb("dev", [P, SLOTS, CHUNKS])
        rstd = sb("rstd", [P, SLOTS, CHUNKS])
        shift = sb("shift", [P, SLOTS, CHUNKS])
        agg_t = sb("agg_t", [P, KD, width])
        ident = sb("ident", [P, P])
        iota_i = sb("iota_i", [P, WIN], I32)
        iota = sb("iota", [P, WIN])
        ones = sb("ones", [1, P])
        eps = sb("eps", [P, 1])
        first_i = sb("first_i", [P, windows], I32)
        first = sb("first", [P, windows])
        x_sb = sb("x_sb", [P, tiles, dim])
        gw_sb = sb("gw_sb", [P, KD, dim])
        b1_all = sb("b1_all", [P, experts, FB])
        b1_rows = sb("b1_rows", [experts * FB, P])
        b2_sb = sb("b2_sb", [experts, dim])
        wr_sb = sb("wr_sb", [P, KD, experts])
        br_sb = sb("br_sb", [1, experts])
        gb_row = sb("gb_row", [1, 2 * dim])
        gb = sb("gb", [P, 2 * dim])
        g_key = sb("g_key", [P, CHUNKS])
        g_idx = sb("g_idx", [P, 1], I32)
        g_hit = sb("g_hit", [P, 2])
        agg_tile = sb("agg_tile", [P, TILE_SLOTS, KD, P])
        z_tile = sb("z_tile", [P, TILE_SLOTS, dim])
        t_stats = sb("t_stats", [P, TILE_SLOTS, 6])
        t_dev = sb("t_dev", [P, tiles])
        t_mv = sb("t_mv", [P, TILE_SLOTS, 2])
        z_rstd = sb("z_rstd", [P, tiles])
        z_shift = sb("z_shift", [P, tiles])
        col_part = sb("col_part", [P, KD, tiles])
        col_sum = sb("col_sum", [P, KD])
        logit = sb("logit", [1, experts])
        r_exp = sb("r_exp", [1, experts])
        r_w = sb("r_w", [1, experts])
        r_load = sb("r_load", [1, experts])
        r_scale = sb("r_scale", [1, experts])
        r_flag = sb("r_flag", [1, experts])
        r_s = sb("r_s", [1, 8])
        top_v = sb("top_v", [1, 8])
        top_i = sb("top_i", [1, 8], U32)
        top_if = sb("top_if", [1, 8])
        top_w = sb("top_w", [1, 2])
        dense = sb("dense", [1, 2, experts])
        dense_b = sb("dense_b", [experts, P])
        top_wb = sb("top_wb", [P, 2])
        bias_b = sb("bias_b", [P, dim])
        w1_s = sb("w1_s", [P, 2, KD, hidden])
        w2_s = sb("w2_s", [P, 2, FB, dim])
        b1_s = sb("b1_s", [P, 2, FB])
        hT = ring[:, 0:2 * 2 * FB * SPAN].rearrange("p (b e f n) -> p b e f n", b=2, e=2, f=FB)
        res = sb("res", [P, 2, dim])
        o_t = sb("o_t", [P, 2, dim])
        o_n = sb("o_n", [P, 2, dim])
        f_stats = sb("f_stats", [P, 2, 6])
        f_mv = sb("f_mv", [P, 2, 2])
        f_rstd = sb("f_rstd", [P, 2])
        f_shift = sb("f_shift", [P, 2])
        f_var = sb("f_var", [P, 2])
        f_root = sb("f_root", [P, 2])
        f_corr = sb("f_corr", [P, 2])
        y_out = sb("y_out", [P, 2, 4, dim])

        ps = [ctx.enter_context(nc.psum_tensor(f"ps{i}", [P, 512], F32)) for i in range(3)]
        ps_sum = [ctx.enter_context(nc.psum_tensor(f"ps_sum{i}", [P, 512], F32)) for i in range(SUM_BANKS)]
        ps_y = ps_sum[0:2]
        ps_r = ctx.enter_context(nc.psum_tensor("ps_r", [P, 512], F32))

        src_in, dst_in, wgt_in = sem("src_in"), sem("dst_in"), sem("wgt_in")
        w1_in, w2_in = [sem("w1_in0"), sem("w1_in1")], [sem("w2_in0"), sem("w2_in1")]
        x_in, gw_in, small_in = sem("x_in"), sem("gw_in"), sem("small_in")
        zeroed = sem("zeroed")
        counted = sem("counted")
        ones_set = sem("ones_set")
        ident_set = sem("ident_set")
        prep = sem("prep")
        turned = sem("turned")
        evacuated = sem("evacuated")
        gathered = [sem(f"gathered{s}") for s in range(SLOTS)]
        slot_ready = sem("slot_ready")
        passed = sem("passed")
        built = sem("built")
        stat = sem("stat")
        shifted = sem("shifted")
        normed = sem("normed")
        summed = sem("summed")
        rooted = sem("rooted")
        scaled = sem("scaled")
        added = sem("added")
        gen_gather, gen_stat, gen_norm = sem("gen_gather"), sem("gen_stat"), sem("gen_norm")
        gen_idx, gen_hot, gen_mm, gen_add = sem("gen_idx"), sem("gen_hot"), sem("gen_mm"), sem("gen_add")
        gen_key, gen_win, gen_rstd = sem("gen_key"), sem("gen_win"), sem("gen_rstd")
        agg_done = sem("agg_done")
        tile_copied, tile_mm, tile_x1, tile_stat = sem("tile_copied"), sem("tile_mm"), sem("tile_x1"), sem("tile_stat")
        tile_r, tile_root, tile_shift, gen_root, gen_shift, root = (sem("tile_r"), sem("tile_root"), sem("tile_shift"),
                                                      sem("gen_root"), sem("gen_shift"), sem("root"))
        tile_z, tile_turned, tile_zt = sem("tile_z"), sem("tile_turned"), sem("tile_zt")
        route_v, route_a, route_p = sem("route_v"), sem("route_a"), sem("route_p")
        picked = sem("picked")
        w2_scaled = sem("w2_scaled")
        l1_done, gelu_done, l2_done = sem("l1_done"), sem("gelu_done"), sem("l2_done")
        res_v, res_p, res_done, x1b = sem("res_v"), sem("res_p"), sem("res_done"), sem("x1b")
        o_v, o_a, o_g, o_p = sem("o_v"), sem("o_a"), sem("o_g"), sem("o_p")
        stored = [sem("stored0"), sem("stored1")]

        block = ctx.enter_context(nc.Block())

        @block.sync
        def _(sp):
            sp.wait_ge(zeroed, 1)
            s2 = src[0:full * GROUP].rearrange("(g e) -> g e", e=GROUP)
            d2 = dst[0:full * GROUP].rearrange("(g e) -> g e", e=GROUP)
            e2 = edge_weight[0:full * GROUP].rearrange("(g e) -> g e", e=GROUP)
            for to, of, flat, done in ((src_rows, s2, src, src_in), (dst_rows, d2, dst, dst_in),
                                       (wgt_rows, e2, edge_weight, wgt_in)):
                sp.dma_start(to[0:even, :], of[0:even, :]).then_inc(done, 16)
                sp.dma_start(to[even:full, :], of[even:full, :]).then_inc(done, 16)
                sp.dma_start(to[full:groups, 0:rest],
                             flat[full * GROUP:edges].rearrange("(a e) -> a e", a=1)).then_inc(done, 16)
            sp.dma_start(dst_rows[full:groups, rest:GROUP],
                         dst[edges - (GROUP - rest):edges].rearrange("(a e) -> a e", a=1)).then_inc(dst_in, 16)
            sp.dma_start(gw_sb[:, :, :], gnn_w.rearrange("(k p) n -> p k n", p=P)).then_inc(gw_in, 16)
            sp.dma_start(wr_sb[:, :, :], wr.rearrange("(k p) n -> p k n", p=P)).then_inc(small_in, 16)
            sp.dma_start(br_sb[:, :], br.rearrange("(a n) -> a n", a=1)).then_inc(small_in, 16)
            sp.dma_start(gb_row[:, 0:dim], gamma.rearrange("(a n) -> a n", a=1)).then_inc(small_in, 16)
            sp.dma_start(gb_row[:, dim:2 * dim], beta.rearrange("(a n) -> a n", a=1)).then_inc(small_in, 16)
            sp.dma_start(b1_rows[:, :], b1.rearrange("e (f p) -> (e f) p", p=P)).then_inc(small_in, 16)
            sp.dma_start(b2_sb[:, :], b2).then_inc(small_in, 16)
            sp.wait_ge(zeroed, 2)
            sp.dma_start(x_sb[:, 0:tiles - 1, :],
                         x[0:(tiles - 1) * P, :].rearrange("(t p) d -> p t d", p=P)).then_inc(x_in, 16)
            sp.dma_start(x_sb[0:tail, tiles - 1, :], x[(tiles - 1) * P:nodes, :]).then_inc(x_in, 16)
            sp.wait_ge(route_v, ROUTE_TOP)
            which = [sp.value_load(top_i[0:1, e:e + 1], min_val=0, max_val=experts - 1) for e in range(2)]
            for e in range(2):
                sp.dma_start(w1_s[:, e, :, :],
                             w1[bass.ds(which[e], 1)].rearrange("a (k p) f -> p (a k) f", p=P)).then_inc(w1_in[e], 16)
            for e in range(2):
                sp.dma_start(w2_s[:, e, :, :],
                             w2[bass.ds(which[e], 1)].rearrange("a (f p) d -> p (a f) d", p=P)).then_inc(w2_in[e], 16)
            with sp.Fori(0, spans // 2) as i:
                for b in range(2):
                    sp.wait_ge(o_p, 8 * i + 4 * b + 4)
                    sp.dma_start(out[bass.ds(2 * SPAN * i + SPAN * b, SPAN), :].rearrange("(t p) d -> p t d", p=P),
                                 y_out[:, b, :, :]).then_inc(stored[b], 16)
            sp.wait_ge(o_p, tiles)
            sp.dma_start(out[spans * SPAN:nodes, :], y_out[0:tail, 0, 0, :]).then_inc(stored[0], 16)
            sp.wait_ge(stored[0], 16 * (spans // 2 + 1))
            sp.wait_ge(stored[1], 16 * (spans // 2))

        @block.gpsimd
        def _(pool):
            pool.memset(ident[:, :], 0.0).then_inc(ident_set, 1)
            pool.wait_ge(ident_set, 1)
            pool.affine_select(out=ident[:, :], in_=ident[:, :], compare_op=ALU.not_equal, fill=1.0, base=0,
                               pattern=[[-1, P]], channel_multiplier=1).then_inc(ident_set, 1)
            pool.iota(iota_i[:, :], pattern=[[1, WIN]], base=0, channel_multiplier=0).then_inc(counted, 1)
            pool.iota(first_i[:, :], pattern=[[WIN, windows]], base=0, channel_multiplier=0).then_inc(counted, 1)

            def gather_group(i, s):
                for c in range(CHUNKS):
                    pool.indirect_dma_start(
                        out=raw[:, s, c, :], out_offset=None, in_=x,
                        in_offset=bass.IndirectOffsetOnAxis(ap=idx_slot[:, s, c:c + 1], axis=0),
                    ).then_inc(gathered[s], 16)

            for s in range(SLOTS):
                pool.wait_ge(slot_ready, s + 1)
                gather_group(0, s)
            with pool.Fori(1, rounds) as i:
                for s in range(SLOTS):
                    pool.wait_ge(slot_ready, SLOTS * i + s + 1)
                    pool.sem_inc(passed, 1)
                    gather_group(i, s)

            pool.wait_ge(prep, PREP_FLAG)
            flag = pool.value_load(behind[0:1, 0:1])
            with pool.If(flag > 0):
                with pool.Fori(0, groups) as g:
                    for c in range(CHUNKS):
                        pool.wait_ge(gen_idx, CHUNKS * g + c + 1)
                        pool.sem_inc(passed, 1)
                        pool.indirect_dma_start(
                            out=raw[:, 0, 0, :], out_offset=None, in_=x,
                            in_offset=bass.IndirectOffsetOnAxis(ap=g_idx[:, 0:1], axis=0),
                        ).then_inc(gen_gather, 16)

            pool.wait_ge(agg_done, 1)
            for s in range(TILE_SLOTS):
                pool.tensor_copy(agg_tile[:, s, :, :], agg_t[:, :, P * s:P * s + P]).then_inc(tile_copied, 1)
            with pool.Fori(1, tile_rounds) as i:
                for s in range(TILE_SLOTS):
                    pool.wait_ge(tile_mm, TILE_SLOTS * (i - 1) + s + 1)
                    pool.tensor_copy(agg_tile[:, s, :, :],
                                     agg_t[:, :, bass.ds(P * TILE_SLOTS * i + P * s, P)]).then_inc(tile_copied, 1)

            pool.wait_ge(route_v, ROUTE_BIAS)

            def residual(n, b):
                pool.wait_ge(res_v, n + 1)
                pool.tensor_tensor(res[:, b, :], res[:, b, :], bias_b[:, :], ALU.add).then_inc(res_p, 1)

            def finish(n, t, b, j, yb, wait_store):
                pool.wait_ge(o_a, n + 1)
                if wait_store is not None:
                    pool.wait_ge(stored[yb], wait_store)
                pool.tensor_tensor(o_n[:, b, :], o_n[:, b, :], gb[:, 0:dim], ALU.mult).then_inc(o_g, 1)
                pool.wait_ge(o_g, n + 1)
                pool.tensor_tensor(y_out[:, yb, j, :], o_n[:, b, :], x_sb[:, t, :] if isinstance(t, int)
                                   else x_sb[:, bass.ds(t, 1), :].rearrange("p a d -> p (a d)"),
                                   ALU.add).then_inc(o_p, 1)

            residual(0, 0)
            for n in range(8):
                residual(n + 1, (n + 1) % 2)
                finish(n, n, n % 2, n % 4, n // 4, None)
            with pool.Fori(1, spans // 2) as i:
                for m in range(8):
                    residual(8 * i + m + 1, (m + 1) % 2)
                    finish(8 * i + m, 8 * i + m, m % 2, m % 4, m // 4, 16 * i if m % 4 == 0 else None)
            finish(tiles - 1, tiles - 1, 0, 0, 0, 16 * (spans // 2))

        @block.scalar
        def _(act):
            def stage_indices(g, s, first):
                at = idx_t[:, g, :] if first else idx_t[:, bass.ds(g, 1), :].rearrange("p a c -> p (a c)")
                act.copy(idx_slot[:, s, :], at).then_inc(slot_ready, 1)

            act.wait_ge(evacuated, CHUNKS)
            for s in range(SLOTS):
                stage_indices(s, s, True)

            def deviation(g, s):
                act.wait_ge(stat, 2 * g + 2)
                act.activation(dev[:, s, :], meanvar[:, s, :, 1], ACT.Sqrt, bias=eps[:, 0:1]).then_inc(rooted, 1)

            def normalise(g, s, first):
                act.wait_ge(shifted, g + 1)
                if not first:
                    act.wait_ge(summed, g - SLOTS + 2)
                for c in range(CHUNKS):
                    act.activation(xn[:, s, c, :], raw[:, s, c, :], ACT.Identity, bias=shift[:, s, c:c + 1],
                                   scale=rstd[:, s, c:c + 1]).then_inc(normed, 1)
                act.wait_ge(normed, CHUNKS * g + CHUNKS)
                stage_indices(g + SLOTS, s, first)

            act.wait_ge(ones_set, 2)
            deviation(0, 0)
            for s in range(1, SLOTS):
                deviation(s, s)
                normalise(s - 1, s - 1, True)
            with act.Fori(1, rounds) as i:
                for s in range(SLOTS):
                    deviation(SLOTS * i + s, s)
                    normalise(SLOTS * i + s - 1, (s - 1) % SLOTS, False)
            normalise(groups - 1, SLOTS - 1, False)

            act.wait_ge(prep, PREP_FLAG)
            flag = act.value_load(behind[0:1, 0:1])
            act.wait_ge(summed, groups)
            with act.If(flag > 0):
                with act.Fori(0, groups) as g:
                    for c in range(CHUNKS):
                        act.wait_ge(gen_mm, windows * CHUNKS * g + windows * c + 1)
                        act.copy(g_idx[:, 0:1], idx_t[:, bass.ds(g, 1), c:c + 1].rearrange("p a c -> p (a c)")
                                 ).then_inc(gen_idx, 1)
                        act.wait_ge(gen_stat, 2 * CHUNKS * g + 2 * c + 2)
                        act.activation(dev[:, 0, 0:1], meanvar[:, 0, 0, 1:2], ACT.Sqrt,
                                       bias=eps[:, 0:1]).then_inc(gen_root, 1)
                        act.wait_ge(gen_shift, CHUNKS * g + c + 1)
                        act.activation(xn[:, 0, 0, :], raw[:, 0, 0, :], ACT.Identity, bias=shift[:, 0, 0:1],
                                       scale=rstd[:, 0, 0:1]).then_inc(gen_norm, 1)

            def root_tile(n, s):
                act.wait_ge(tile_stat, 2 * n + 2)
                act.activation(t_dev[:, bass.ds(n, 1)], t_mv[:, s, 1:2], ACT.Sqrt, bias=eps[:, 0:1]).then_inc(tile_root, 1)

            def norm_tile(n, s, first):
                act.wait_ge(tile_shift, n + 1)
                if not first:
                    act.wait_ge(tile_turned, n - TILE_SLOTS + 2)
                at = bass.ds(n, 1)
                act.activation(z_tile[:, s, :], x_sb[:, at, :].rearrange("p a d -> p (a d)"), ACT.Identity,
                               bias=z_shift[:, at], scale=z_rstd[:, at]).then_inc(tile_z, 1)

            def turn_tile(n, s):
                act.wait_ge(tile_turned, n + 1)
                for k in range(KD):
                    act.activation(agg_t[:, k, bass.ds(P * n, P)], ps[s % 2][:, P * k:P * k + P], ACT.Copy,
                                   accum_out=col_part[:, k, bass.ds(n, 1)]).then_inc(tile_zt, 1)

            for s in range(TILE_SLOTS):
                root_tile(s, s)
                if s >= 1:
                    norm_tile(s - 1, s - 1, True)
                if s >= 2:
                    turn_tile(s - 2, s - 2)
            with act.Fori(1, tile_rounds) as i:
                for s in range(TILE_SLOTS):
                    n = TILE_SLOTS * i + s
                    root_tile(n, s)
                    norm_tile(n - 1, (s - 1) % TILE_SLOTS, False)
                    turn_tile(n - 2, (s - 2) % TILE_SLOTS)
            norm_tile(tiles - 1, TILE_SLOTS - 1, False)
            turn_tile(tiles - 2, TILE_SLOTS - 2)
            turn_tile(tiles - 1, TILE_SLOTS - 1)

            act.wait_ge(route_v, ROUTE_MAX0)
            act.activation(r_exp[:, :], logit[:, :], ACT.Exp, bias=r_s[:, 0:1], accum_out=r_s[:, 1:2]).then_inc(route_a, 1)
            act.wait_ge(route_v, ROUTE_MAX1)
            act.activation(r_exp[:, :], r_load[:, :], ACT.Exp, bias=r_s[:, 2:3], accum_out=r_s[:, 3:4]).then_inc(route_a, 1)
            act.wait_ge(route_v, ROUTE_TOP)
            act.activation(top_w[:, :], top_v[:, 0:2], ACT.Exp, bias=r_s[:, 4:5], accum_out=r_s[:, 5:6]).then_inc(route_a, 1)

            for e in range(2):
                which = act.value_load(top_i[0:1, e:e + 1], min_val=0, max_val=experts - 1)
                act.copy(b1_s[:, e, :], b1_all[:, bass.ds(which, 1), :].rearrange("p a f -> p (a f)")
                         ).then_inc(picked, 1)

            act.wait_ge(picked, PICKED)

            def gelu_span(q, buf, free, cols=SPAN):
                for e in range(2):
                    for f in range(FB):
                        m = e * FB + f
                        act.wait_ge(l1_done, 2 * FB * q + m + 1)
                        if m == 0 and free is not None:
                            act.wait_ge(l2_done, free)
                        act.activation(hT[:, buf, e, f, 0:cols], ps[m % 2][:, 0:cols], ACT.Gelu,
                                       bias=b1_s[:, e, f:f + 1]).then_inc(gelu_done, 1)

            def norm_out(n, b):
                act.wait_ge(o_v, 3 * n + 3)
                act.activation(o_n[:, b, :], o_t[:, b, :], ACT.Identity, bias=f_shift[:, b:b + 1],
                               scale=f_rstd[:, b:b + 1]).then_inc(o_a, 1)

            def norm_outs(q):
                for j in range(4):
                    n = 4 * q + j
                    if not (isinstance(n, int) and n < 2):
                        act.wait_ge(o_p, n - 1)
                    norm_out(n, j % 2)

            gelu_span(0, 0, None)
            gelu_span(1, 1, None)
            norm_outs(0)
            with act.Fori(1, spans // 2) as i:
                gelu_span(2 * i, 0, 8 * i - 4)
                norm_outs(2 * i - 1)
                gelu_span(2 * i + 1, 1, 8 * i)
                norm_outs(2 * i)
            gelu_span(spans, 0, 4 * spans - 4, TAILW)
            norm_outs(spans - 1)
            act.wait_ge(o_p, tiles - 2)
            norm_out(tiles - 1, 0)

        @block.tensor
        def _(pe):
            pe.wait_ge(ident_set, 2)
            n = 0
            for rows, ready in ((src_f, PREP_SRC), (rel_f, PREP_REL), (wgt_rows, None), (dst_f, None)):
                if ready is None and rows is wgt_rows:
                    pe.wait_ge(wgt_in, 48)
                elif ready is not None:
                    pe.wait_ge(prep, ready)
                for c in range(CHUNKS):
                    if n >= 3:
                        pe.wait_ge(evacuated, n - 2)
                    pe.transpose(ps[n % 3][:, 0:groups], rows[0:groups, c * P:c * P + P],
                                 ident[0:groups, 0:groups]).then_inc(turned, 1)
                    n += 1
            pe.transpose(ps_r[0:1, 0:groups], g_min[0:groups, :], ident[0:groups, 0:groups]).then_inc(turned, 1)
            pe.transpose(ps_r[0:1, P:P + groups], g_max[0:groups, :], ident[0:groups, 0:groups]).then_inc(turned, 1)
            pe.wait_ge(small_in, 16 * 6)
            pe.wait_ge(ones_set, 1)
            pe.matmul(ps_y[0][:, 0:2 * dim], ones[:, :], gb_row[:, :], start=True, stop=True).then_inc(turned, 1)
            pe.transpose(ps_y[1][:, 0:experts * FB], b1_rows[:, :],
                         ident[0:experts * FB, 0:experts * FB]).then_inc(turned, 1)

            pe.wait_ge(prep, PREP_ALL)

            def sum_group(i, s, first):
                g = SLOTS * i + s
                pe.wait_ge(built, CHUNKS * g + CHUNKS)
                if not (first and s < SUM_GAP):
                    pe.wait_ge(added, g - SUM_GAP + 1)
                pe.wait_ge(normed, CHUNKS * g + CHUNKS)
                for k in range(KD):
                    for c in range(CHUNKS):
                        mm = pe.matmul(ps_sum[s % SUM_BANKS][:, WIN * k:WIN * k + WIN],
                                       xn[:, s, c, P * k:P * k + P], onehot[:, s, c, :],
                                       start=(c == 0), stop=(c == CHUNKS - 1))
                mm.then_inc(summed, 1)

            for s in range(SLOTS):
                sum_group(0, s, True)
            with pe.Fori(1, rounds) as i:
                for s in range(SLOTS):
                    sum_group(i, s, False)

            pe.wait_ge(prep, PREP_FLAG)
            flag = pe.value_load(behind[0:1, 0:1])
            with pe.If(flag > 0):
                pe.sem_inc(gen_mm, 1)
                with pe.Fori(0, groups) as g:
                    for c in range(CHUNKS):
                        pe.wait_ge(gen_norm, CHUNKS * g + c + 1)
                        pe.sem_inc(passed, 1)
                        with pe.Fori(0, windows) as v:
                            step = windows * CHUNKS * g + windows * c + v
                            pe.wait_ge(gen_hot, step + 1)
                            for k in range(KD):
                                mm = pe.matmul(ps_sum[0][:, WIN * k:WIN * k + WIN], xn[:, 0, 0, P * k:P * k + P],
                                               onehot[:, 0, 0, :], start=True, stop=True)
                            mm.then_inc(gen_mm, 1)

            pe.wait_ge(gw_in, 16)

            def project(i, s, bank_free):
                n = TILE_SLOTS * i + s
                pe.wait_ge(tile_copied, n + 1)
                if bank_free is not None:
                    pe.wait_ge(tile_x1, bank_free)
                for k in range(KD):
                    mm = pe.matmul(ps_y[s % 2][:, 0:dim], agg_tile[:, s, k, :], gw_sb[:, k, :],
                                   start=(k == 0), stop=(k == KD - 1))
                mm.then_inc(tile_mm, 1)

            def turn(i, s, bank_free):
                n = TILE_SLOTS * i + s
                pe.wait_ge(tile_z, n + 1)
                if bank_free is not None:
                    pe.wait_ge(tile_zt, bank_free)
                for k in range(KD):
                    mm = pe.transpose(ps[s % 2][:, P * k:P * k + P], z_tile[:, s, P * k:P * k + P], ident[:, :])
                mm.then_inc(tile_turned, 1)

            for s in range(TILE_SLOTS):
                project(0, s, s - 1 if s >= 2 else None)
                if s >= 2:
                    turn(0, s - 2, 2 * (s - 2 - 1) if s - 2 >= 2 else None)
            with pe.Fori(1, tile_rounds) as i:
                for s in range(TILE_SLOTS):
                    project(i, s, TILE_SLOTS * i + s - (1 if s else 0))
                    m = s - 2
                    if m >= 0:
                        turn(i, m, 2 * TILE_SLOTS * i + 2 * m - (2 if m else 0))
                    else:
                        m += TILE_SLOTS
                        turn(i - 1, m, 2 * TILE_SLOTS * (i - 1) + 2 * m - 2)
            for m in (TILE_SLOTS - 2, TILE_SLOTS - 1):
                turn(tile_rounds - 1, m, 2 * (TILE_SLOTS * (tile_rounds - 1) + m) - 2)

            pe.wait_ge(route_v, ROUTE_COLS)
            for k in range(KD):
                mm = pe.matmul(ps_r[0:1, 0:experts], col_sum[:, k:k + 1], wr_sb[:, k, :],
                               start=(k == 0), stop=(k == KD - 1))
            mm.then_inc(route_p, 1)
            pe.wait_ge(route_v, ROUTE_DENSE)
            pe.matmul(ps_r[:, 16:18], ones[:, :], top_w[:, :], start=True, stop=True).then_inc(route_p, 1)
            pe.matmul(ps_r[0:experts, P:2 * P], dense[:, 0, :], ones[:, :], start=True, stop=True).then_inc(route_p, 1)
            pe.wait_ge(route_v, ROUTE_DENSE + 2)
            pe.matmul(ps_r[:, 256:256 + dim], dense_b[:, :], b2_sb[:, :], start=True, stop=True).then_inc(route_p, 1)

            def layer1(q, cols, at, first):
                for m in range(2 * FB):
                    e, f = m // FB, m % FB
                    if first and f == 0:
                        pe.wait_ge(w1_in[e], 16)
                    if not (first and m < 2):
                        pe.wait_ge(gelu_done, 2 * FB * q + m - 1)
                    for k in range(KD):
                        mm = pe.matmul(ps[m % 2][:, 0:cols], w1_s[:, e, k, f * P:f * P + P], agg_t[:, k, at],
                                       start=(k == 0), stop=(k == KD - 1))
                    mm.then_inc(l1_done, 1)

            def layer2(q, buf, n_tiles, first):
                if first:
                    pe.wait_ge(w2_scaled, 2)
                pe.wait_ge(gelu_done, 2 * FB * q + 2 * FB)
                for j in range(n_tiles):
                    rows = P if n_tiles == 4 else TAILW
                    if not (first and j < 2):
                        pe.wait_ge(res_done, 4 * q + j - 1)
                    for m in range(2 * FB):
                        e, f = m // FB, m % FB
                        mm = pe.matmul(ps_y[j % 2][0:rows, 0:dim], hT[:, buf, e, f, j * P:j * P + rows],
                                       w2_s[:, e, f, :], start=(m == 0), stop=(m == 2 * FB - 1))
                    mm.then_inc(l2_done, 1)

            layer1(0, SPAN, slice(0, SPAN), True)
            layer1(1, SPAN, slice(SPAN, 2 * SPAN), False)
            layer2(0, 0, 4, True)
            with pe.Fori(1, spans // 2) as i:
                layer1(2 * i, SPAN, bass.ds(2 * SPAN * i, SPAN), False)
                layer2(2 * i - 1, 1, 4, False)
                layer1(2 * i + 1, SPAN, bass.ds(2 * SPAN * i + SPAN, SPAN), False)
                layer2(2 * i, 0, 4, False)
            layer1(spans, TAILW, slice(spans * SPAN, spans * SPAN + TAILW), False)
            layer2(spans - 1, 1, 4, False)
            layer2(spans, 0, 1, False)

        @block.vector
        def _(dve):
            dve.memset(src_rows[:, :], 0)
            dve.memset(wgt_rows[:, :], 0.0).then_inc(zeroed, 1)
            dve.memset(x_sb[:, tiles - 1, :], 0.0).then_inc(zeroed, 1)
            dve.memset(ones[:, :], 1.0).then_inc(ones_set, 1)
            dve.memset(eps[:, :], EPS).then_inc(ones_set, 1)
            dve.memset(idx_t[:, groups:groups + SLOTS, :], 0)
            dve.wait_ge(src_in, 48)
            dve.tensor_copy(src_f[0:groups, :], src_rows[0:groups, :]).then_inc(prep, 1)
            dve.wait_ge(dst_in, 64)
            dve.tensor_copy(dst_f[0:groups, :], dst_rows[0:groups, :]).then_inc(prep, 1)
            for c in range(CHUNKS):
                dve.wait_ge(turned, c + 1)
                dve.tensor_copy(idx_t[:, 0:groups, c], ps[c % 3][:, 0:groups]).then_inc(evacuated, 1)
            dve.wait_ge(prep, 2)
            dve.tensor_reduce(g_min[0:groups, :], dst_f[0:groups, :], AX.X, ALU.min).then_inc(prep, 1)
            dve.tensor_reduce(g_max[0:groups, :], dst_f[0:groups, :], AX.X, ALU.max).then_inc(prep, 1)
            dve.wait_ge(prep, 4)
            dve.tensor_scalar(rel_f[0:groups, :], dst_f[0:groups, :], g_min[0:groups, :], None,
                              ALU.subtract).then_inc(prep, 1)
            dve.wait_ge(counted, 2)
            dve.tensor_copy(iota[:, :], iota_i[:, :]).then_inc(counted, 1)
            dve.tensor_copy(first[:, :], first_i[:, :]).then_inc(counted, 1)
            n = CHUNKS
            for to in (rel_t, wgt_t, dst_t):
                for c in range(CHUNKS):
                    dve.wait_ge(turned, n + 1)
                    dve.tensor_copy(to[:, :, c], ps[n % 3][:, 0:groups]).then_inc(evacuated, 1)
                    n += 1
            dve.wait_ge(turned, n + 2)
            dve.tensor_copy(base_i[:, 0:groups], ps_r[0:1, 0:groups]).then_inc(prep, 1)
            dve.tensor_copy(span_row[:, 0:groups], ps_r[0:1, P:P + groups]).then_inc(prep, 1)
            dve.wait_ge(prep, 7)
            dve.tensor_tensor(span_row[:, 0:groups], span_row[:, 0:groups], ps_r[0:1, 0:groups],
                              ALU.subtract).then_inc(prep, 1)
            dve.wait_ge(prep, 8)
            dve.tensor_reduce(span_max[:, :], span_row[:, 0:groups], AX.X, ALU.max).then_inc(prep, 1)
            dve.wait_ge(prep, 9)
            dve.tensor_scalar(behind[:, :], span_max[:, :], float(WIN), None, ALU.is_ge).then_inc(prep, 1)
            dve.wait_ge(turned, n + 4)
            dve.tensor_copy(gb[:, :], ps_y[0][:, 0:2 * dim]).then_inc(prep, 1)
            dve.tensor_copy(b1_all[:, :, :].rearrange("p e f -> p (e f)"), ps_y[1][:, 0:experts * FB]).then_inc(prep, 1)
            dve.memset(agg_t[:, :, :], 0.0).then_inc(prep, 1)
            dve.wait_ge(prep, PREP_ALL)
            dve.wait_ge(counted, 4)

            def build(i, s, first):
                g = SLOTS * i + s
                if not first:
                    dve.wait_ge(summed, SLOTS * (i - 1) + s + 1)
                for c in range(CHUNKS):
                    at = bass.ds(g, 1)
                    dve.tensor_scalar(onehot[:, s, c, :], iota[:, :], rel_t[:, at, c:c + 1].rearrange("p a c -> p (a c)"),
                                      wgt_t[:, at, c:c + 1].rearrange("p a c -> p (a c)"),
                                      ALU.is_equal, ALU.mult).then_inc(built, 1)

            def statistics(i, s):
                g = SLOTS * i + s
                dve.wait_ge(gathered[s], 16 * CHUNKS * (i + 1))
                for c in range(CHUNKS):
                    bn = dve.bn_stats(bstats[:, s, c, :], raw[:, s, c, :])
                bn.then_inc(stat, 1)
                dve.wait_ge(stat, 2 * g + 1)
                dve.sem_inc(passed, 1)
                for c in range(CHUNKS):
                    bn = dve.bn_aggr(meanvar[:, s, c, :], bstats[:, s, c, :])
                bn.then_inc(stat, 1)

            def scales(g, s):
                dve.wait_ge(rooted, g + 1)
                dve.reciprocal(rstd[:, s, :], dev[:, s, :]).then_inc(scaled, 1)
                dve.wait_ge(scaled, g + 1)
                dve.scalar_tensor_tensor(out=shift[:, s, :], in0=meanvar[:, s, :, 0], scalar=-1.0,
                                         in1=rstd[:, s, :], op0=ALU.mult, op1=ALU.mult).then_inc(shifted, 1)

            def add_sums(g, s):
                dve.wait_ge(summed, g + 1)
                base = dve.value_load(base_i[0:1, g:g + 1] if isinstance(g, int) else base_i[0:1, bass.ds(g, 1)],
                                      min_val=0, max_val=nodes - 1)
                if not (isinstance(g, int) and g == 0):
                    dve.wait_ge(added, g)
                window = agg_t[:, :, bass.ds(base, WIN)]
                dve.tensor_tensor(window, window,
                                  ps_sum[s % SUM_BANKS][:, 0:KD * WIN].rearrange("p (k w) -> p k w", k=KD), ALU.add).then_inc(added, 1)

            for s in range(SLOTS):
                build(0, s, True)
                statistics(0, s)
                if s >= 1:
                    scales(s - 1, s - 1)
                if s >= LAG:
                    add_sums(s - LAG, s - LAG)
            with dve.Fori(1, rounds) as i:
                for s in range(SLOTS):
                    build(i, s, False)
                    statistics(i, s)
                    scales(SLOTS * i + s - 1, (s - 1) % SLOTS)
                    add_sums(SLOTS * i + s - LAG, (s - LAG) % SLOTS)
            scales(groups - 1, SLOTS - 1)
            for g in range(groups - LAG, groups):
                add_sums(g, g % SLOTS)

            flag = dve.value_load(behind[0:1, 0:1])
            with dve.If(flag > 0):
                with dve.Fori(0, groups) as g:
                    gat = bass.ds(g, 1)
                    rel_g = rel_t[:, gat, :].rearrange("p a c -> p (a c)")
                    dst_g = dst_t[:, gat, :].rearrange("p a c -> p (a c)")
                    dve.tensor_scalar(g_key[:, :], rel_g, float(WIN), None, ALU.is_ge).then_inc(gen_key, 1)
                    dve.wait_ge(gen_key, 3 * g + 1)
                    dve.scalar_tensor_tensor(out=g_key[:, :], in0=dst_g, scalar=1.0, in1=g_key[:, :],
                                             op0=ALU.add, op1=ALU.mult).then_inc(gen_key, 1)
                    dve.wait_ge(gen_key, 3 * g + 2)
                    dve.tensor_scalar(g_key[:, :], g_key[:, :], -1.0, None, ALU.add).then_inc(gen_key, 1)
                    dve.wait_ge(gen_key, 3 * g + 3)
                    for c in range(CHUNKS):
                        done = CHUNKS * g + c
                        dve.wait_ge(gen_gather, 16 * done + 16)
                        dve.bn_stats(bstats[:, 0, 0, :], raw[:, 0, 0, :]).then_inc(gen_stat, 1)
                        dve.wait_ge(gen_stat, 2 * done + 1)
                        dve.sem_inc(passed, 1)
                        dve.bn_aggr(meanvar[:, 0, 0, :], bstats[:, 0, 0, :]).then_inc(gen_stat, 1)
                        dve.wait_ge(gen_root, done + 1)
                        dve.reciprocal(rstd[:, 0, 0:1], dev[:, 0, 0:1]).then_inc(gen_rstd, 1)
                        dve.wait_ge(gen_rstd, done + 1)
                        dve.scalar_tensor_tensor(out=shift[:, 0, 0:1], in0=meanvar[:, 0, 0, 0:1], scalar=-1.0,
                                                 in1=rstd[:, 0, 0:1], op0=ALU.mult, op1=ALU.mult).then_inc(gen_shift, 1)
                        with dve.Fori(0, windows) as v:
                            step = windows * done + v
                            dve.tensor_scalar(g_hit[:, 0:1], g_key[:, c:c + 1], first[:, bass.ds(v, 1)], None,
                                              ALU.subtract).then_inc(gen_win, 1)
                            dve.wait_ge(gen_win, step + 1)
                            dve.tensor_scalar(onehot[:, 0, 0, :], iota[:, :], g_hit[:, 0:1],
                                              wgt_t[:, gat, c:c + 1].rearrange("p a c -> p (a c)"),
                                              ALU.is_equal, ALU.mult).then_inc(gen_hot, 1)
                            dve.wait_ge(gen_mm, step + 2)
                            window = agg_t[:, :, bass.ds(WIN * v, WIN)]
                            dve.tensor_tensor(window, window, ps_sum[0][:, 0:KD * WIN].rearrange("p (k w) -> p k w", k=KD),
                                              ALU.add).then_inc(gen_add, 1)
                            dve.wait_ge(gen_add, step + 1)
            dve.wait_ge(added, groups)
            dve.memset(f_shift[:, :], 0.0).then_inc(agg_done, 1)

            dve.wait_ge(x_in, 32)

            def tile(n, s):
                xt = x_sb[:, bass.ds(n, 1), :].rearrange("p a d -> p (a d)")
                dve.wait_ge(tile_mm, n + 1)
                dve.tensor_tensor(xt, xt, ps_y[s % 2][:, 0:dim], ALU.add).then_inc(tile_x1, 1)
                dve.wait_ge(tile_x1, n + 1)
                dve.sem_inc(passed, 1)
                dve.bn_stats(t_stats[:, s, :], xt).then_inc(tile_stat, 1)
                dve.wait_ge(tile_stat, 2 * n + 1)
                dve.sem_inc(passed, 1)
                dve.bn_aggr(t_mv[:, s, :], t_stats[:, s, :]).then_inc(tile_stat, 1)

            def tile_scale(n, s):
                at = bass.ds(n, 1)
                dve.wait_ge(tile_root, n + 1)
                dve.reciprocal(z_rstd[:, at], t_dev[:, at]).then_inc(tile_r, 1)
                dve.wait_ge(tile_r, n + 1)
                dve.scalar_tensor_tensor(out=z_shift[:, at], in0=t_mv[:, s, 0:1], scalar=-1.0, in1=z_rstd[:, at],
                                         op0=ALU.mult, op1=ALU.mult).then_inc(tile_shift, 1)

            for s in range(TILE_SLOTS):
                tile(s, s)
                if s >= 1:
                    tile_scale(s - 1, s - 1)
            with dve.Fori(1, tile_rounds) as i:
                for s in range(TILE_SLOTS):
                    tile(TILE_SLOTS * i + s, s)
                    tile_scale(TILE_SLOTS * i + s - 1, (s - 1) % TILE_SLOTS)
            tile_scale(tiles - 1, TILE_SLOTS - 1)

            count = [0]

            def step(ins):
                count[0] += 1
                ins.then_inc(route_v, 1)
                dve.wait_ge(route_v, count[0])

            dve.wait_ge(tile_zt, 2 * tiles)
            step(dve.tensor_reduce(col_sum[:, :], col_part[:, :, :], AX.X, ALU.add))
            step(dve.tensor_scalar(col_sum[:, :], col_sum[:, :], 1.0 / nodes, None, ALU.mult))
            assert count[0] == ROUTE_COLS
            dve.wait_ge(small_in, 16 * 6)
            dve.wait_ge(route_p, 1)
            step(dve.tensor_tensor(logit[:, :], ps_r[0:1, 0:experts], br_sb[:, :], ALU.add))
            step(dve.tensor_reduce(r_s[:, 0:1], logit[:, :], AX.X, ALU.max))
            step(dve.tensor_scalar(r_s[:, 0:1], r_s[:, 0:1], -1.0, None, ALU.mult))
            assert count[0] == ROUTE_MAX0
            dve.wait_ge(route_a, 1)
            step(dve.reciprocal(r_s[:, 1:2], r_s[:, 1:2]))
            step(dve.tensor_scalar(r_w[:, :], r_exp[:, :], r_s[:, 1:2], None, ALU.mult))
            step(dve.tensor_scalar(r_load[:, :], r_w[:, :], float(nodes), None, ALU.mult))
            step(dve.tensor_scalar(r_flag[:, :], r_load[:, :], capacity, None, ALU.is_gt))
            step(dve.reciprocal(r_scale[:, :], r_load[:, :]))
            step(dve.scalar_tensor_tensor(out=r_scale[:, :], in0=r_scale[:, :], scalar=capacity, in1=r_flag[:, :],
                                          op0=ALU.mult, op1=ALU.mult))
            step(dve.tensor_scalar(r_flag[:, :], r_flag[:, :], -1.0, 1.0, ALU.mult, ALU.add))
            step(dve.tensor_tensor(r_scale[:, :], r_scale[:, :], r_flag[:, :], ALU.add))
            step(dve.tensor_tensor(r_load[:, :], r_w[:, :], r_scale[:, :], ALU.mult))
            step(dve.tensor_reduce(r_s[:, 2:3], r_load[:, :], AX.X, ALU.max))
            step(dve.tensor_scalar(r_s[:, 2:3], r_s[:, 2:3], -1.0, None, ALU.mult))
            assert count[0] == ROUTE_MAX1
            dve.wait_ge(route_a, 2)
            step(dve.reciprocal(r_s[:, 3:4], r_s[:, 3:4]))
            step(dve.tensor_scalar(r_w[:, :], r_exp[:, :], r_s[:, 3:4], None, ALU.mult))
            step(dve.max(top_v[:, :], r_w[:, :]))
            step(dve.max_index(top_i[:, :], top_v[:, :], r_w[:, :]))
            step(dve.tensor_scalar(r_s[:, 4:5], top_v[:, 0:1], -1.0, None, ALU.mult))
            assert count[0] == ROUTE_TOP
            dve.wait_ge(route_a, 3)
            step(dve.reciprocal(r_s[:, 5:6], r_s[:, 5:6]))
            step(dve.tensor_scalar(top_w[:, :], top_w[:, :], r_s[:, 5:6], None, ALU.mult))
            step(dve.tensor_copy(top_if[:, :], top_i[:, :]))
            for e in range(2):
                step(dve.tensor_scalar(dense[:, e, :], iota[0:1, 0:experts], top_if[:, e:e + 1], top_w[:, e:e + 1],
                                       ALU.is_equal, ALU.mult))
            step(dve.tensor_tensor(dense[:, 0, :], dense[:, 0, :], dense[:, 1, :], ALU.add))
            assert count[0] == ROUTE_DENSE
            dve.wait_ge(route_p, 3)
            step(dve.tensor_copy(top_wb[:, :], ps_r[:, 16:18]))
            step(dve.tensor_copy(dense_b[:, :], ps_r[0:experts, P:2 * P]))
            dve.wait_ge(route_p, 4)
            step(dve.tensor_copy(bias_b[:, :], ps_r[:, 256:256 + dim]))
            for e in range(2):
                dve.wait_ge(w2_in[e], 16)
                dve.tensor_scalar(w2_s[:, e, :, :], w2_s[:, e, :, :], top_wb[:, e:e + 1], None,
                                  ALU.mult).then_inc(w2_scaled, 1)
            assert count[0] == ROUTE_BIAS

            def make_res(n, b):
                at = bass.ds(n, 1)
                dve.tensor_scalar(res[:, b, :], x_sb[:, at, :].rearrange("p a d -> p (a d)"), z_rstd[:, at],
                                  z_shift[:, at], ALU.mult, ALU.add).then_inc(res_v, 1)

            def newton(n, k, ins):
                ins.then_inc(root, 1)
                dve.wait_ge(root, NEWTON_STEPS * n + k + 1)

            def out_tile(n, b, first):
                at = bass.ds(n, 1)
                dve.wait_ge(res_p, n + 1)
                dve.wait_ge(l2_done, n + 1)
                if not first:
                    dve.wait_ge(o_a, n - 1)
                dve.tensor_tensor(o_t[:, b, :], res[:, b, :], ps_y[b][:, 0:dim], ALU.add).then_inc(res_done, 1)
                dve.wait_ge(res_done, n + 1)
                dve.sem_inc(passed, 1)
                dve.bn_stats(f_stats[:, b, :], o_t[:, b, :]).then_inc(o_v, 1)
                dve.wait_ge(o_v, 3 * n + 1)
                dve.sem_inc(passed, 1)
                dve.bn_aggr(f_mv[:, b, :], f_stats[:, b, :]).then_inc(o_v, 1)
                dve.wait_ge(o_v, 3 * n + 2)
                v, y, e = f_var[:, b:b + 1], f_root[:, b:b + 1], f_corr[:, b:b + 1]
                newton(n, 0, dve.tensor_scalar(v, f_mv[:, b, 1:2], EPS, None, ALU.add))
                newton(n, 1, dve.tensor_scalar(y.bitcast(I32), v.bitcast(I32), 1, None, ALU.logical_shift_right))
                newton(n, 2, dve.tensor_scalar(y.bitcast(I32), y.bitcast(I32), -1.0, ROOT_MAGIC, ALU.mult, ALU.add))
                for k in range(NEWTON):
                    newton(n, 3 + 3 * k, dve.scalar_tensor_tensor(out=e, in0=y, scalar=v, in1=y, op0=ALU.mult,
                                                                  op1=ALU.mult))
                    newton(n, 4 + 3 * k, dve.tensor_scalar(e, e, -0.5, 1.5, ALU.mult, ALU.add))
                    to = f_rstd[:, b:b + 1] if k == NEWTON - 1 else y
                    newton(n, 5 + 3 * k, dve.tensor_tensor(to, y, e, ALU.mult))
                xt = x_sb[:, at, :].rearrange("p a d -> p (a d)")
                dve.tensor_tensor(xt, xt, gb[:, dim:2 * dim], ALU.add).then_inc(x1b, 1)
                dve.wait_ge(x1b, n + 1)
                dve.scalar_tensor_tensor(out=f_shift[:, b:b + 1], in0=f_mv[:, b, 0:1], scalar=-1.0,
                                         in1=f_rstd[:, b:b + 1], op0=ALU.mult, op1=ALU.mult).then_inc(o_v, 1)

            make_res(0, 0)
            for n in range(8):
                out_tile(n, n % 2, n < 2)
                make_res(n + 1, (n + 1) % 2)
            with dve.Fori(1, spans // 2) as i:
                for m in range(8):
                    out_tile(8 * i + m, m % 2, False)
                    make_res(8 * i + m + 1, (m + 1) % 2)
            out_tile(tiles - 1, 0, False)


_INS = ["x", "src", "dst", "edge_weight", "L0_gnn_weight", "L0_ffn_Wr", "L0_ffn_br", "L0_ffn_W1", "L0_ffn_b1",
        "L0_ffn_W2", "L0_ffn_b2", "L0_ffn_gamma", "L0_ffn_beta"]


def kernel(**inputs):
    import numpy as _np
    import concourse.bacc as _bacc
    from concourse import mybir as _mybir
    from concourse.bass_utils import run_bass_kernel_spmd as _run

    nc = _bacc.Bacc("TRN2", target_bir_lowering=False, num_devices=1)
    arrays, args = {}, []
    for name in _INS:
        a = _np.ascontiguousarray(inputs[name])
        arrays[f"in_{name}_dram"] = a
        args.append(nc.dram_tensor(f"in_{name}_dram", a.shape, _mybir.dt.from_np(a.dtype), kind="ExternalInput").ap())
    out = nc.dram_tensor("out_0_dram", inputs["x"].shape, _mybir.dt.float32, kind="ExternalOutput").ap()
    gnn_moe(nc, *args, out)
    r = _run(nc, [arrays], core_ids=[0])
    return r.results[0]["out_0_dram"]
```

```python
import math
from contextlib import ExitStack

import concourse.bass as bass
from concourse import mybir

ALU = mybir.AluOpType
ACT = mybir.ActivationFunctionType
AX = mybir.AxisListType
F32 = mybir.dt.float32
F32R = mybir.dt.float32r
I32 = mybir.dt.int32
U32 = mybir.dt.uint32

P = 128
EPS = 1e-5
CHUNKS = 4
GROUP = CHUNKS * P
WIN = 40
SLOTS = 7
SUM_BANKS = 4
SUM_GAP = 3
LAG = 3
POOL_TILES = 2
FUSE = 3
FUSE_SLOT = 2
SPAN_TILES = 3
TILE_AFTER = (2, 5, 7)
SUM_AFTER = (3, 6, 7)
CAPACITY_FACTOR = 1.25

PREP_SRC, PREP_REL, PREP_FLAG, PREP_ALL = 1, 5, 13, 17
ROUTE_COLS, ROUTE_MAX0, ROUTE_MAX1, ROUTE_TOP, ROUTE_PAIR, ROUTE_DENSE, ROUTE_BIAS = 1, 4, 12, 16, 17, 23, 26
ROOT_MAGIC = float(0x5F3759DF)
NEWTON = 3
NEWTON_STEPS = 3 + 4 * NEWTON


def gnn_moe(nc, x, src, dst, edge_weight, gnn_w, wr, br, w1, b1, w2, b2, gamma, beta, table, out):
    nodes, dim = x.shape
    edges = src.shape[0]
    experts, _, hidden = w1.shape
    KD = dim // P
    FB = hidden // P
    HB = 2 * FB
    groups = -(-edges // GROUP)
    full = edges // GROUP
    rest = edges - full * GROUP
    even = full // 16 * 16
    rounds = groups // SLOTS
    assert groups == rounds * SLOTS and groups == full + 1 and groups <= P
    tiles = -(-nodes // P)
    tail = nodes - (tiles - 1) * P
    batches = [(0, 7), (7, 14), (14, 20), (20, tiles)]
    width = tiles * P
    assert nodes - 1 + WIN <= width
    windows = width // WIN
    pairs = tiles // 2
    early = rounds - FUSE
    late = [(k, min(2, tiles - 2 * k), (k - early + 1) % 2) for k in range(early, pairs + 1)]
    assert len(late) == 2 and tiles == 2 * pairs + 1
    first_checked = SLOTS * FUSE + FUSE_SLOT - LAG
    assert first_checked + SLOTS * early == groups - 1
    SPAN = SPAN_TILES * P
    spans = tiles // SPAN_TILES
    assert tiles == spans * SPAN_TILES + 1 and spans % 2 == 0
    tiles_up = (spans + 1) * SPAN_TILES
    capacity = float(math.ceil(nodes * CAPACITY_FACTOR / experts))

    with ExitStack() as ctx:
        def sb(name, shape, dt=F32):
            return ctx.enter_context(nc.sbuf_tensor(name, shape, dt))

        def sem(name):
            return ctx.enter_context(nc.semaphore(name))

        agg_t = sb("agg_t", [P, KD, width])
        x_sb = sb("x_sb", [P, tiles_up, dim])
        zt_h = sb("zt_h", [P, KD, width], F32R)
        zt_l = sb("zt_l", [P, KD, width], F32R)
        z_rstd = sb("z_rstd", [P, tiles_up])
        z_shift = sb("z_shift", [P, tiles_up])
        ident = sb("ident", [P, P])
        regular = sb("regular", [1, 1], I32)
        iota = sb("iota", [P, WIN])
        ones = sb("ones", [1, P])
        ones_col = sb("ones_col", [P, 1])
        eps = sb("eps", [P, 1])
        b1_all = sb("b1_all", [P, experts, FB])
        b2_sb = sb("b2_sb", [experts, dim])
        wr_sb = sb("wr_sb", [P, KD, experts])
        br_sb = sb("br_sb", [1, experts])
        gb = sb("gb", [P, 2 * dim])
        bias_b = sb("bias_b", [P, dim])
        col_mean = sb("col_mean", [P, KD])
        logit = sb("logit", [1, experts])
        r_exp = sb("r_exp", [1, experts])
        r_w = sb("r_w", [1, experts])
        r_scale = sb("r_scale", [1, experts])
        r_s = sb("r_s", [1, 8])
        top_v = sb("top_v", [1, 8])
        top_i = sb("top_i", [1, 8], U32)
        top_if = sb("top_if", [1, 8])
        top_w = sb("top_w", [1, 2])
        dense = sb("dense", [1, 2, experts])
        dense_b = sb("dense_b", [experts, P])
        top_wb = sb("top_wb", [P, 2])
        b1_s = sb("b1_s", [P, 2, FB])
        spare = sb("spare", [1, 2])
        f_stats = sb("f_stats", [P, SPAN_TILES, 6])
        f_mv = sb("f_mv", [P, SPAN_TILES, 2])
        f_var = sb("f_var", [P, SPAN_TILES])
        f_root = sb("f_root", [P, SPAN_TILES])
        f_corr = sb("f_corr", [P, SPAN_TILES])
        f_rstd = sb("f_rstd", [P, SPAN_TILES])
        f_shift = sb("f_shift", [P, SPAN_TILES])

        with ExitStack() as early_ctx:
            def sb1(name, shape, dt=F32):
                return early_ctx.enter_context(nc.sbuf_tensor(name, shape, dt))

            g_min = sb1("g_min", [P, 1])
            g_max = sb1("g_max", [P, 1])
            base_i = sb1("base_i", [1, P], I32)
            base_f = sb1("base_f", [1, P])
            need_i = sb1("need_i", [1, P], I32)
            need_f = sb1("need_f", [1, P])
            span_row = sb1("span_row", [1, P])
            room_row = sb1("room_row", [1, P])
            worst = sb1("worst", [1, 3])
            idx_t = sb1("idx_t", [P, groups + SLOTS, CHUNKS], I32)
            rel_t = sb1("rel_t", [P, groups, CHUNKS])
            wgt_t = sb1("wgt_t", [P, groups, CHUNKS])
            dst_t = sb1("dst_t", [P, groups, CHUNKS])
            idx_slot = sb1("idx_slot", [P, SLOTS, CHUNKS], I32)
            raw = sb1("raw", [P, SLOTS, CHUNKS, dim])
            x_h = sb1("x_h", [P, SUM_BANKS, CHUNKS, dim], F32R)
            x_l = sb1("x_l", [P, SUM_BANKS, CHUNKS, dim], F32R)
            xn = raw[:, :, :, :].rearrange("p s c d -> p (s c d)")[:, 0:tiles * dim].rearrange(
                "p (t d) -> p t d", t=tiles)
            prepare = agg_t[:, :, :].rearrange("p k n -> p (k n)")[:, 0:6 * GROUP].rearrange("p (n e) -> p n e", n=6)
            src_rows, dst_rows = (prepare[:, n, :].bitcast(I32) for n in range(2))
            wgt_rows, src_f, dst_f = (prepare[:, n, :] for n in range(2, 5))
            rel_f = prepare[:, 5, :]
            onehot = sb1("onehot", [P, SUM_BANKS, CHUNKS, WIN], F32R)
            n_stats = sb1("n_stats", [P, tiles, 6])
            n_mv = sb1("n_mv", [P, tiles, 2])
            n_dev = sb1("n_dev", [P, tiles])
            n_rstd = sb1("n_rstd", [P, tiles])
            n_shift = sb1("n_shift", [P, tiles])
            iota_i = sb1("iota_i", [P, WIN], I32)
            first_i = sb1("first_i", [P, windows], I32)
            first = sb1("first", [P, windows])
            g_key = sb1("g_key", [P, CHUNKS])
            g_idx = sb1("g_idx", [P, 1], I32)
            g_hit = sb1("g_hit", [P, 1])
            gw_sb = sb1("gw_sb", [P, KD, dim])
            gb_row = sb1("gb_row", [1, 2 * dim])
            b1_rows = sb1("b1_rows", [experts * FB, P])
            agg_pair = sb1("agg_pair", [P, 2, KD, 2 * P])
            z_pair = sb1("z_pair", [P, 2, 2, dim])
            t_stats = sb1("t_stats", [P, 2, 2, 6])
            t_mv = sb1("t_mv", [P, 2, 2, 2])
            t_dev = sb1("t_dev", [P, 2, 2])
            zero2 = sb1("zero2", [P, KD])

        w1_h = sb("w1_h", [P, 2, KD, hidden], F32R)
        w1_l = sb("w1_l", [P, 2, KD, hidden], F32R)
        w2_h = sb("w2_h", [P, 2, FB, dim], F32R)
        w2_l = sb("w2_l", [P, 2, FB, dim], F32R)
        h_h = sb("h_h", [P, 2, HB, SPAN], F32R)
        h_l = sb("h_l", [P, 2, HB, SPAN], F32R)
        h_x = sb("h_x", [P, 2, SPAN])
        y_out = sb("y_out", [P, 2, SPAN_TILES, dim])
        y_last = sb("y_last", [P, dim])
        flat = agg_t[:, :, :].rearrange("p k n -> p (k n)")
        W1N, W2N, RN = 2 * KD * hidden, 2 * FB * dim, 2 * SPAN_TILES * dim
        w1_raw = flat[:, 0:W1N].rearrange("p (e k f) -> p e k f", e=2, k=KD)
        w2_raw = flat[:, W1N:W1N + W2N].rearrange("p (e f d) -> p e f d", e=2, f=FB)
        res = flat[:, W1N + W2N:W1N + W2N + RN].rearrange("p (b t d) -> p b t d", b=2, t=SPAN_TILES)
        o_t = flat[:, 0:RN].rearrange("p (b t d) -> p b t d", b=2, t=SPAN_TILES)

        ps = [ctx.enter_context(nc.psum_tensor(f"ps{i}", [P, 512], F32)) for i in range(3)]
        ps_sum = [ctx.enter_context(nc.psum_tensor(f"ps_sum{i}", [P, 512], F32)) for i in range(SUM_BANKS)]
        ps_r = ctx.enter_context(nc.psum_tensor("ps_r", [P, 512], F32))
        ps_project = [ps[0], ps[2]]
        ps_turn = [ps[1], ps_sum[0]]
        ps_hidden = ps + [ps_r]

        src_in, dst_in, wgt_in, gw_in, small_in = (sem(n) for n in (
            "src_in", "dst_in", "wgt_in", "gw_in", "small_in"))
        x_in = [sem(f"x_in{j}") for j in range(len(batches))]
        n_stat = sem("n_stat")
        n_rooted = sem("n_rooted")
        n_scaled = sem("n_scaled")
        n_act, n_pool = sem("n_act"), sem("n_pool")
        table_in = sem("table_in")
        w1_in, w2_in = [sem("w1_in0"), sem("w1_in1")], [sem("w2_in0"), sem("w2_in1")]
        zeroed = sem("zeroed")
        counted = sem("counted")
        constants = sem("constants")
        ident_set = sem("ident_set")
        prep = sem("prep")
        turned = sem("turned")
        evacuated = sem("evacuated")
        gathered = [sem(f"gathered{s}") for s in range(SLOTS)]
        slot_ready = sem("slot_ready")
        passed = sem("passed")
        built = sem("built")
        x_high = sem("x_high")
        x_low = sem("x_low")
        summed = sem("summed")
        added = sem("added")
        gen_gather, gen_high, gen_low = sem("gen_gather"), sem("gen_high"), sem("gen_low")
        gen_idx, gen_hot, gen_mm, gen_add = sem("gen_idx"), sem("gen_hot"), sem("gen_mm"), sem("gen_add")
        gen_key, gen_win, gen_done = sem("gen_key"), sem("gen_win"), sem("gen_done")
        copied = sem("copied")
        projected = sem("projected")
        x1_made = sem("x1_made")
        t_stat = sem("t_stat")
        t_rooted = sem("t_rooted")
        t_scaled = sem("t_scaled")
        z_made = sem("z_made")
        z_turned = sem("z_turned")
        z_high = sem("z_high")
        z_low = sem("z_low")
        z_counted = sem("z_counted")
        route_v, route_a, route_p = sem("route_v"), sem("route_a"), sem("route_p")
        b1_picked = sem("b1_picked")
        w1_high, w1_low, w2_scaled, w2_high, w2_low = (sem(n) for n in (
            "w1_high", "w1_low", "w2_scaled", "w2_high", "w2_low"))
        l1_done = sem("l1_done")
        gelu_done = sem("gelu_done")
        h_low = sem("h_low")
        l2_done = sem("l2_done")
        res_made = sem("res_made")
        res_biased = sem("res_biased")
        o_made = sem("o_made")
        o_stat = sem("o_stat")
        f_shifted = sem("f_shifted")
        root = sem("root")
        o_normed = sem("o_normed")
        x1_beta = sem("x1_beta")
        y_gamma, y_made = sem("y_gamma"), sem("y_made")
        last_gamma, last_made = sem("last_gamma"), sem("last_made")
        stored = [sem("stored0"), sem("stored1")]

        block = ctx.enter_context(nc.Block())

        @block.sync
        def _(sp):
            for j, (lo, hi) in enumerate(batches):
                whole = min(hi, tiles - 1)
                sp.dma_start(x_sb[:, lo:whole, :],
                             x[lo * P:whole * P, :].rearrange("(t p) d -> p t d", p=P)).then_inc(x_in[j], 16)
            sp.wait_ge(zeroed, 1)
            sp.dma_start(x_sb[0:tail, tiles - 1, :], x[(tiles - 1) * P:nodes, :]).then_inc(x_in[-1], 16)
            for to, of, done, ready in ((src_rows, src, src_in, 2), (wgt_rows, edge_weight, wgt_in, 3),
                                        (dst_rows, dst, dst_in, None)):
                by_group = of[0:full * GROUP].rearrange("(g e) -> g e", e=GROUP)
                if ready is not None:
                    sp.wait_ge(zeroed, ready)
                sp.dma_start(to[0:even, :], by_group[0:even, :]).then_inc(done, 16)
                sp.dma_start(to[even:full, :], by_group[even:full, :]).then_inc(done, 16)
                sp.dma_start(to[full:groups, 0:rest],
                              of[full * GROUP:edges].rearrange("(a e) -> a e", a=1)).then_inc(done, 16)
            sp.dma_start(dst_rows[full:groups, rest:GROUP],
                          dst[edges - (GROUP - rest):edges].rearrange("(a e) -> a e", a=1)).then_inc(dst_in, 16)
            for j, (lo, hi) in enumerate(batches):
                whole = min(hi, tiles - 1)
                sp.wait_ge(n_act, j + 1)
                sp.wait_ge(n_pool, j + 1)
                sp.dma_start(table[lo * P:whole * P, :].rearrange("(t p) d -> p t d", p=P),
                             xn[:, lo:whole, :]).then_inc(table_in, 16)
            sp.dma_start(table[(tiles - 1) * P:nodes, :], xn[0:tail, tiles - 1, :]).then_inc(table_in, 16)
            sp.dma_start(gb_row[:, 0:dim], gamma.rearrange("(a n) -> a n", a=1)).then_inc(small_in, 16)
            sp.dma_start(gb_row[:, dim:2 * dim], beta.rearrange("(a n) -> a n", a=1)).then_inc(small_in, 16)
            sp.dma_start(b1_rows[:, :], b1.rearrange("e (f p) -> (e f) p", p=P)).then_inc(small_in, 16)
            sp.dma_start(wr_sb[:, :, :], wr.rearrange("(k p) n -> p k n", p=P)).then_inc(small_in, 16)
            sp.dma_start(br_sb[:, :], br.rearrange("(a n) -> a n", a=1)).then_inc(small_in, 16)
            sp.dma_start(b2_sb[:, :], b2).then_inc(small_in, 16)
            sp.dma_start(gw_sb[:, :, :], gnn_w.rearrange("(k p) n -> p k n", p=P)).then_inc(gw_in, 16)
            sp.wait_ge(route_v, ROUTE_TOP)
            which = [sp.value_load(top_i[0:1, e:e + 1], min_val=0, max_val=experts - 1) for e in range(2)]
            for e in range(2):
                sp.dma_start(w1_raw[:, e, :, :],
                             w1[bass.ds(which[e], 1)].rearrange("a (k p) f -> p (a k) f", p=P)).then_inc(w1_in[e], 16)
            for e in range(2):
                sp.dma_start(w2_raw[:, e, :, :],
                             w2[bass.ds(which[e], 1)].rearrange("a (f p) d -> p (a f) d", p=P)).then_inc(w2_in[e], 16)
            def store(q, b):
                sp.dma_start(out[bass.ds(SPAN * q, SPAN), :].rearrange("(t p) d -> p t d", p=P),
                             y_out[:, b, :, :]).then_inc(stored[b], 16)

            with sp.Fori(0, spans // 2 - 1) as i:
                for b in range(2):
                    sp.wait_ge(y_made, 2 * i + b + 1)
                    store(2 * i + b, b)
            sp.wait_ge(y_made, spans - 1)
            store(spans - 2, 0)
            sp.wait_ge(last_made, 1)
            store(spans - 1, 1)
            sp.wait_ge(last_made, 2)
            sp.dma_start(out[spans * SPAN:nodes, :], y_last[0:tail, :]).then_inc(stored[0], 16)
            sp.wait_ge(stored[0], 16 * (spans // 2 + 1))
            sp.wait_ge(stored[1], 16 * (spans // 2))

        @block.gpsimd
        def _(pool):
            pool.memset(ident[:, :], 0.0).then_inc(ident_set, 1)
            pool.wait_ge(ident_set, 1)
            pool.affine_select(out=ident[:, :], in_=ident[:, :], compare_op=ALU.not_equal, fill=1.0, base=0,
                               pattern=[[-1, P]], channel_multiplier=1).then_inc(ident_set, 1)
            pool.iota(iota_i[:, :], pattern=[[1, WIN]], base=0, channel_multiplier=0).then_inc(counted, 1)
            pool.iota(first_i[:, :], pattern=[[WIN, windows]], base=0, channel_multiplier=0).then_inc(counted, 1)
            pool.iota(need_i[:, 0:SLOTS * (early + 1)], pattern=[[2 * P, early + 1], [0, SLOTS]], base=2 * P,
                      channel_multiplier=0).then_inc(counted, 1)

            for j, (lo, hi) in enumerate(batches):
                pool.wait_ge(n_scaled, 2 * j + 2)
                for t in range(hi - POOL_TILES, hi):
                    a = pool.tensor_scalar(xn[:, t, :], x_sb[:, t, :], n_rstd[:, t:t + 1], n_shift[:, t:t + 1],
                                           ALU.mult, ALU.add)
                a.then_inc(n_pool, 1)

            def gather_group(s):
                for c in range(CHUNKS):
                    pool.indirect_dma_start(
                        out=raw[:, s, c, :], out_offset=None, in_=table,
                        in_offset=bass.IndirectOffsetOnAxis(ap=idx_slot[:, s, c:c + 1], axis=0),
                    ).then_inc(gathered[s], 16)

            pool.wait_ge(table_in, 16 * (len(batches) + 1))
            for s in range(SLOTS):
                pool.wait_ge(slot_ready, s + 1)
                gather_group(s)
            with pool.Fori(1, rounds) as i:
                for s in range(SLOTS):
                    pool.wait_ge(slot_ready, SLOTS * i + s + 1)
                    pool.sem_inc(passed, 1)
                    gather_group(s)

            pool.wait_ge(prep, PREP_FLAG)
            flag = pool.value_load(regular[0:1, 0:1])
            with pool.If(flag < 1):
                with pool.Fori(0, groups) as g:
                    for c in range(CHUNKS):
                        pool.wait_ge(gen_idx, CHUNKS * g + c + 1)
                        pool.sem_inc(passed, 1)
                        pool.indirect_dma_start(
                            out=raw[:, 0, 0, :], out_offset=None, in_=table,
                            in_offset=bass.IndirectOffsetOnAxis(ap=g_idx[:, 0:1], axis=0),
                        ).then_inc(gen_gather, 16)

            def over(a, n):
                return a.unsqueeze(1).to_broadcast([P, n, dim])

            def add_bias(q, b, n):
                pool.wait_ge(res_made, q + 1)
                pool.tensor_tensor(res[:, b, 0:n, :], res[:, b, 0:n, :], over(bias_b[:, :], n),
                                   ALU.add).then_inc(res_biased, 1)
                at = x_sb[:, SPAN_TILES * q:SPAN_TILES * q + n, :] if isinstance(q, int) else \
                    x_sb[:, bass.ds(SPAN_TILES * q, n), :]
                pool.tensor_tensor(at, at, over(gb[:, dim:2 * dim], n), ALU.add).then_inc(x1_beta, 1)

            def finish(q, b, n, stores):
                y, at = y_out[:, b, 0:n, :], x_sb[:, bass.ds(SPAN_TILES * q, n), :]
                if stores is not None:
                    pool.wait_ge(stored[b], stores)
                pool.wait_ge(o_normed, q + 1)
                pool.tensor_tensor(y, o_t[:, b, 0:n, :], over(gb[:, 0:dim], n), ALU.mult).then_inc(y_gamma, 1)
                pool.wait_ge(y_gamma, q + 2)
                pool.tensor_tensor(y, y, at, ALU.add).then_inc(y_made, 1)

            pool.wait_ge(route_v, ROUTE_BIAS)
            pool.sem_inc(y_gamma, 1)
            for q in range(3):
                add_bias(q, q % 2, SPAN_TILES)
            finish(0, 0, SPAN_TILES, None)
            add_bias(3, 1, SPAN_TILES)
            finish(1, 1, SPAN_TILES, None)
            add_bias(4, 0, SPAN_TILES)
            with pool.Fori(1, spans // 2 - 1) as i:
                for b in range(2):
                    finish(2 * i + b, b, SPAN_TILES, 16 * i)
                    add_bias(2 * i + b + 3, 1 - b, SPAN_TILES)
            finish(spans - 2, 0, SPAN_TILES, 16 * (spans // 2 - 1))

        @block.scalar
        def _(act):
            act.wait_ge(constants, 4)

            def root_batch(j):
                lo, hi = batches[j]
                act.wait_ge(n_stat, 2 * j + 2)
                act.activation(n_dev[:, lo:hi], n_mv[:, lo:hi, 1], ACT.Sqrt, bias=eps[:, 0:1]).then_inc(n_rooted, 1)

            def norm_batch(j):
                act.wait_ge(n_scaled, 2 * j + 2)
                for t in range(batches[j][0], batches[j][1] - POOL_TILES):
                    a = act.activation(xn[:, t, :], x_sb[:, t, :], ACT.Identity, bias=n_shift[:, t:t + 1],
                                       scale=n_rstd[:, t:t + 1])
                a.then_inc(n_act, 1)

            root_batch(0)
            for j in range(1, len(batches)):
                root_batch(j)
                norm_batch(j - 1)
            norm_batch(len(batches) - 1)

            def high_rows(i, s, first):
                if not (first and s < SUM_GAP):
                    act.wait_ge(summed, SLOTS * i + s - SUM_GAP + 1)
                act.wait_ge(gathered[s], 16 * CHUNKS * (i + 1))
                if not first:
                    act.sem_inc(passed, 1)
                at = bass.ds(SLOTS * i + s, 1)
                for c in range(CHUNKS):
                    a = act.activation(x_h[:, s % SUM_BANKS, c, :], raw[:, s, c, :], ACT.Copy,
                                       scale=wgt_t[:, at, c:c + 1].rearrange("p a c -> p (a c)"))
                a.then_inc(x_high, 1)

            def copy_pair(k, n, b):
                if isinstance(k, int) and k >= early:
                    act.wait_ge(projected, k - 1)
                act.copy(agg_pair[:, b, :, 0:n * P], agg_t[:, :, bass.ds(2 * P * k, n * P)]).then_inc(copied, 1)

            def root_pair(k, n, b):
                act.wait_ge(t_stat, 2 * k + 2)
                act.activation(t_dev[:, b, 0:n], t_mv[:, b, 0:n, 1], ACT.Sqrt, bias=eps[:, 0:1]).then_inc(t_rooted, 1)

            def norm_pair(k, n, b):
                act.wait_ge(t_scaled, 2 * k + 2)
                if isinstance(k, int) and k >= early:
                    act.wait_ge(z_turned, k - 1)
                for t in range(n):
                    at = bass.ds(2 * k + t, 1)
                    a = act.activation(z_pair[:, b, t, :], x_sb[:, at, :].rearrange("p a d -> p (a d)"),
                                       ACT.Identity, bias=z_shift[:, at], scale=z_rstd[:, at])
                a.then_inc(z_made, 1)

            def high_pair(k, n, b):
                act.wait_ge(z_turned, k + 1)
                act.copy(zt_h[:, :, bass.ds(2 * P * k, n * P)],
                         ps_turn[b][:, 0:KD * n * P].rearrange("p (k n) -> p k n", k=KD)).then_inc(z_high, 1)

            act.wait_ge(evacuated, 3 * CHUNKS)
            for s in range(SLOTS):
                high_rows(0, s, True)
            with act.Fori(1, FUSE) as i:
                for s in range(SLOTS):
                    high_rows(i, s, False)
            act.wait_ge(prep, PREP_FLAG)
            flag = act.value_load(regular[0:1, 0:1])
            def act_fused(i, first):
                for s in range(SLOTS):
                    high_rows(i, s, False)
                    if s == 1 and not first:
                        high_pair(i - FUSE - 1, 2, 0)
                    if s == FUSE_SLOT:
                        act.wait_ge(added, SLOTS * i + s - LAG)
                        act.sem_inc(passed, 1)
                        copy_pair(i - FUSE, 2, 0)
                    if s == 5:
                        root_pair(i - FUSE, 2, 0)
                    if s == 6:
                        norm_pair(i - FUSE, 2, 0)

            with act.If(flag > 0):
                act_fused(FUSE, True)
                with act.Fori(FUSE + 1, rounds) as i:
                    act_fused(i, False)
                high_pair(early - 1, 2, 0)
            with act.Else():
                with act.Fori(FUSE, rounds) as i:
                    for s in range(SLOTS):
                        high_rows(i, s, False)
                act.wait_ge(summed, groups)
                with act.Fori(0, groups) as g:
                    for c in range(CHUNKS):
                        act.wait_ge(gen_mm, windows * CHUNKS * g + windows * c + 1)
                        act.copy(g_idx[:, 0:1], idx_t[:, bass.ds(g, 1), c:c + 1].rearrange("p a c -> p (a c)")
                                 ).then_inc(gen_idx, 1)
                        act.wait_ge(gen_gather, 16 * CHUNKS * g + 16 * c + 16)
                        act.sem_inc(passed, 1)
                        act.activation(x_h[:, 0, 0, :], raw[:, 0, 0, :], ACT.Copy,
                                       scale=wgt_t[:, bass.ds(g, 1), c:c + 1].rearrange("p a c -> p (a c)")
                                       ).then_inc(gen_high, 1)
                act.wait_ge(gen_done, 1)
                with act.Fori(0, early) as k:
                    copy_pair(k, 2, 0)
                    root_pair(k, 2, 0)
                    norm_pair(k, 2, 0)
                    high_pair(k, 2, 0)
            q, r = late
            act.wait_ge(added, groups - 1)
            copy_pair(*q)
            act.wait_ge(added, groups)
            for stage, pair in ((copy_pair, r), (root_pair, q), (norm_pair, q), (root_pair, r), (norm_pair, r),
                                (high_pair, q), (high_pair, r)):
                stage(*pair)

            act.activation(spare[:, 0:1], eps[0:1, :], ACT.Exp)
            act.wait_ge(route_v, ROUTE_MAX0)
            act.activation(r_exp[:, :], logit[:, :], ACT.Exp, accum_out=r_s[:, 1:2]).then_inc(route_a, 1)
            act.wait_ge(route_v, ROUTE_MAX1)
            act.activation(r_exp[:, :], r_w[:, :], ACT.Exp, accum_out=r_s[:, 3:4]).then_inc(route_a, 1)
            act.wait_ge(route_v, ROUTE_PAIR)
            act.activation(top_w[:, :], r_s[:, 6:8], ACT.Exp, accum_out=r_s[:, 5:6]).then_inc(route_a, 1)
            act.activation(spare[:, 1:2], eps[0:1, :], ACT.Gelu)
            for e in range(2):
                which = act.value_load(top_i[0:1, e:e + 1], min_val=0, max_val=experts - 1)
                act.copy(b1_s[:, e, :], b1_all[:, bass.ds(which, 1), :].rearrange("p a f -> p (a f)")
                         ).then_inc(b1_picked, 1)
            for e in range(2):
                act.wait_ge(w1_in[e], 16)
                act.copy(w1_h[:, e, :, :], w1_raw[:, e, :, :]).then_inc(w1_high, 1)
            act.wait_ge(b1_picked, 2)

            def gelu_span(q, b, cols, free):
                for m in range(HB):
                    n = HB * q + m
                    if m == 0 and free is not None:
                        act.wait_ge(l2_done, free)
                    act.wait_ge(l1_done, n + 1)
                    bias = b1_s[:, m // FB, m % FB:m % FB + 1]
                    act.activation(h_h[:, b, m, 0:cols], ps_hidden[m % 4][:, 0:cols], ACT.Gelu, bias=bias)
                    if not (isinstance(n, int) and n < 2):
                        act.wait_ge(h_low, n - 1)
                    act.activation(h_x[:, m % 2, 0:cols], ps_hidden[m % 4][:, 0:cols], ACT.Gelu,
                                   bias=bias).then_inc(gelu_done, 1)

            gelu_span(0, 0, SPAN, None)
            for e in range(2):
                act.wait_ge(w2_scaled, e + 1)
                act.copy(w2_h[:, e, :, :], w2_raw[:, e, :, :]).then_inc(w2_high, 1)
            gelu_span(1, 1, SPAN, None)
            with act.Fori(1, spans // 2) as i:
                for b in range(2):
                    gelu_span(2 * i + b, b, SPAN, SPAN_TILES * (2 * i + b - 1))
            gelu_span(spans, 0, P, SPAN_TILES * (spans - 1))

        @block.tensor
        def _(pe):
            pe.wait_ge(ident_set, 2)
            n = 0
            for rows, wait in ((src_f, (prep, PREP_SRC)), (rel_f, (prep, PREP_REL)), (wgt_rows, (wgt_in, 48)),
                               (dst_f, None)):
                if wait is not None:
                    pe.wait_ge(*wait)
                for c in range(CHUNKS):
                    if n >= 3:
                        pe.wait_ge(evacuated, n - 2)
                    pe.transpose(ps[n % 3][:, 0:groups], rows[0:groups, c * P:c * P + P],
                                 ident[0:groups, 0:groups]).then_inc(turned, 1)
                    n += 1
            pe.transpose(ps_r[0:1, 0:groups], g_min[0:groups, :], ident[0:groups, 0:groups]).then_inc(turned, 1)
            pe.transpose(ps_r[0:1, P:P + groups], g_max[0:groups, :], ident[0:groups, 0:groups]).then_inc(turned, 1)
            pe.wait_ge(small_in, 16 * 6)
            pe.wait_ge(constants, 4)
            pe.matmul(ps_sum[0][:, 0:2 * dim], ones[:, :], gb_row[:, :], start=True, stop=True).then_inc(turned, 1)
            pe.transpose(ps_sum[1][:, 0:experts * FB], b1_rows[:, :],
                         ident[0:experts * FB, 0:experts * FB]).then_inc(turned, 1)
            pe.wait_ge(prep, PREP_ALL)
            pe.matmul(ps_r[:, 0:KD], ident[:, :], zero2[:, :], start=True, stop=False, skip_group_check=True)

            def sum_group(i, s, first):
                g = SLOTS * i + s
                pe.wait_ge(built, g + 1)
                if not (first and s < SUM_GAP):
                    pe.wait_ge(added, g - SUM_GAP + 1)
                pe.wait_ge(x_low, g + 1)
                for k in range(KD):
                    n = 0
                    for part in (x_h, x_l):
                        for c in range(CHUNKS):
                            mm = pe.matmul(ps_sum[s % SUM_BANKS][:, WIN * k:WIN * k + WIN],
                                           part[:, s % SUM_BANKS, c, P * k:P * k + P], onehot[:, s % SUM_BANKS, c, :],
                                           start=(n == 0), stop=(n == 2 * CHUNKS - 1))
                            n += 1
                mm.then_inc(summed, 1)

            def project(k, n, b):
                pe.wait_ge(copied, k + 1)
                if isinstance(k, int) and k >= early:
                    pe.wait_ge(x1_made, k - 1)
                for t in range(n):
                    for h in range(KD):
                        mm = pe.matmul(ps_project[b][:, dim * t:dim * t + dim], agg_pair[:, b, h, P * t:P * t + P],
                                       gw_sb[:, h, :], start=(h == 0), stop=(h == KD - 1))
                mm.then_inc(projected, 1)

            def turn(k, n, b, last=False):
                pe.wait_ge(z_made, k + 1)
                if isinstance(k, int) and k >= early:
                    pe.wait_ge(z_low, k - 1)
                for t in range(n):
                    for h in range(KD):
                        at = P * (n * h + t)
                        mm = pe.transpose(ps_turn[b][:, at:at + P], z_pair[:, b, t, P * h:P * h + P], ident[:, :])
                mm.then_inc(z_turned, 1)
                for t in range(n):
                    for h in range(KD):
                        mm = pe.matmul(ps_r[:, h:h + 1], z_pair[:, b, t, P * h:P * h + P], ones_col[:, :],
                                       start=False, stop=(last and t == n - 1), skip_group_check=True)
                mm.then_inc(z_counted, 1)

            for s in range(SLOTS):
                sum_group(0, s, True)
            with pe.Fori(1, FUSE) as i:
                for s in range(SLOTS):
                    sum_group(i, s, False)
            pe.wait_ge(gw_in, 16)
            flag = pe.value_load(regular[0:1, 0:1])
            with pe.If(flag > 0):
                with pe.Fori(FUSE, rounds) as i:
                    for s in range(SLOTS):
                        sum_group(i, s, False)
                        if s == FUSE_SLOT:
                            project(i - FUSE, 2, 0)
                        if s == 6:
                            turn(i - FUSE, 2, 0)
            with pe.Else():
                with pe.Fori(FUSE, rounds) as i:
                    for s in range(SLOTS):
                        sum_group(i, s, False)
                pe.sem_inc(gen_mm, 1)
                with pe.Fori(0, groups) as g:
                    for c in range(CHUNKS):
                        pe.wait_ge(gen_low, CHUNKS * g + c + 1)
                        pe.sem_inc(passed, 1)
                        with pe.Fori(0, windows) as v:
                            step = windows * CHUNKS * g + windows * c + v
                            pe.wait_ge(gen_hot, step + 1)
                            for k in range(KD):
                                for part in (x_h, x_l):
                                    mm = pe.matmul(ps_sum[0][:, WIN * k:WIN * k + WIN],
                                                   part[:, 0, 0, P * k:P * k + P], onehot[:, 0, 0, :],
                                                   start=(part is x_h), stop=(part is x_l))
                            mm.then_inc(gen_mm, 1)
                with pe.Fori(0, early) as k:
                    project(k, 2, 0)
                    turn(k, 2, 0)
            q, r = late
            project(*q)
            project(*r)
            turn(*q)
            turn(*r, last=True)

            pe.wait_ge(route_v, ROUTE_COLS)
            for k in range(KD):
                mm = pe.matmul(ps_r[0:1, 8:8 + experts], col_mean[:, k:k + 1], wr_sb[:, k, :],
                               start=(k == 0), stop=(k == KD - 1))
            mm.then_inc(route_p, 1)
            pe.wait_ge(route_v, ROUTE_DENSE)
            pe.matmul(ps_r[:, 16:18], ones[:, :], top_w[:, :], start=True, stop=True).then_inc(route_p, 1)
            pe.matmul(ps_r[0:experts, P:2 * P], dense[:, 0, :], ones[:, :], start=True, stop=True).then_inc(route_p, 1)
            pe.wait_ge(route_v, ROUTE_DENSE + 2)
            pe.matmul(ps_r[:, 256:256 + dim], dense_b[:, :], b2_sb[:, :], start=True, stop=True).then_inc(route_p, 1)

            def block1(q, m, cols, at, first):
                e, f = m // FB, m % FB
                if first and f == 0:
                    pe.wait_ge(w1_low, e + 1)
                if first and m == 3:
                    pe.wait_ge(route_v, ROUTE_BIAS)
                if not (first and m < 4):
                    pe.wait_ge(gelu_done, HB * q + m - 3)
                n = 0
                for wt, z in ((w1_h, zt_h), (w1_h, zt_l), (w1_l, zt_h)):
                    for k in range(KD):
                        mm = pe.matmul(ps_hidden[m % 4][:, 0:cols], wt[:, e, k, f * P:f * P + P], z[:, k, at],
                                       start=(n == 0), stop=(n == 3 * KD - 1))
                        n += 1
                mm.then_inc(l1_done, 1)

            def tile2(q, b, j, first):
                if first and j == 0:
                    pe.wait_ge(w2_low, 2)
                if j == 0:
                    pe.wait_ge(h_low, HB * q + HB)
                if not (first and j < 2):
                    pe.wait_ge(o_made, SPAN_TILES * q + j - 1)
                n = 0
                for h, wt in ((h_h, w2_h), (h_h, w2_l), (h_l, w2_h)):
                    for m in range(HB):
                        mm = pe.matmul(ps_sum[(SPAN_TILES * b + j) % SUM_BANKS][:, 0:dim],
                                       h[:, b, m, j * P:j * P + P], wt[:, m // FB, m % FB, :],
                                       start=(n == 0), stop=(n == 3 * HB - 1))
                        n += 1
                mm.then_inc(l2_done, 1)

            def layers(q, b, cols, at, first=False):
                for m in range(HB):
                    block1(q, m, cols, at, False)
                    if m in TILE_AFTER:
                        tile2(q - 1, 1 - b, TILE_AFTER.index(m), first)

            for m in range(HB):
                block1(0, m, SPAN, slice(0, SPAN), True)
            layers(1, 1, SPAN, slice(SPAN, 2 * SPAN), first=True)
            with pe.Fori(1, spans // 2) as i:
                for b in range(2):
                    layers(2 * i + b, b, SPAN, bass.ds(2 * SPAN * i + SPAN * b, SPAN))
            layers(spans, 0, P, slice(spans * SPAN, spans * SPAN + P))
            tile2(spans, 0, 0, False)

        @block.vector
        def _(dve):
            dve.memset(x_sb[:, tiles - 1:tiles_up, :], 0.0).then_inc(zeroed, 1)
            dve.memset(src_rows[96:P, :], 0).then_inc(zeroed, 1)
            dve.memset(wgt_rows[96:P, :], 0.0).then_inc(zeroed, 1)
            dve.memset(ones[:, :], 1.0).then_inc(constants, 1)
            dve.memset(eps[:, :], EPS).then_inc(constants, 1)
            dve.memset(zero2[:, :], 0.0).then_inc(constants, 1)
            dve.memset(ones_col[:, :], 1.0).then_inc(constants, 1)
            dve.memset(z_rstd[:, :], 0.0)
            dve.memset(z_shift[:, :], 0.0)
            dve.memset(idx_t[:, groups:groups + SLOTS, :], 0)

            def stat_batch(j):
                lo, hi = batches[j]
                dve.wait_ge(x_in[j], 32 if hi == tiles else 16)
                for t in range(lo, hi):
                    bn = dve.bn_stats(n_stats[:, t, :], x_sb[:, t, :])
                bn.then_inc(n_stat, 1)
                dve.wait_ge(n_stat, 2 * j + 1)
                for t in range(lo, hi):
                    bn = dve.bn_aggr(n_mv[:, t, :], n_stats[:, t, :])
                bn.then_inc(n_stat, 1)

            def scale_batch(j):
                lo, hi = batches[j]
                dve.wait_ge(n_rooted, j + 1)
                dve.reciprocal(n_rstd[:, lo:hi], n_dev[:, lo:hi]).then_inc(n_scaled, 1)
                dve.wait_ge(n_scaled, 2 * j + 1)
                dve.scalar_tensor_tensor(out=n_shift[:, lo:hi], in0=n_mv[:, lo:hi, 0], scalar=-1.0,
                                         in1=n_rstd[:, lo:hi], op0=ALU.mult, op1=ALU.mult).then_inc(n_scaled, 1)

            stat_batch(0)
            for j in range(1, len(batches)):
                stat_batch(j)
                scale_batch(j - 1)
            dve.wait_ge(src_in, 48)
            dve.tensor_copy(src_f[0:groups, :], src_rows[0:groups, :]).then_inc(prep, 1)
            scale_batch(len(batches) - 1)
            for c in range(CHUNKS):
                dve.wait_ge(turned, c + 1)
                dve.tensor_copy(idx_t[:, 0:groups, c], ps[c % 3][:, 0:groups]).then_inc(evacuated, 1)
            dve.wait_ge(evacuated, CHUNKS)
            for s in range(SLOTS):
                dve.tensor_copy(idx_slot[:, s, :], idx_t[:, s, :]).then_inc(slot_ready, 1)
            dve.wait_ge(dst_in, 64)
            dve.tensor_copy(dst_f[0:groups, :], dst_rows[0:groups, :]).then_inc(prep, 1)
            dve.wait_ge(prep, 2)
            dve.tensor_reduce(g_min[0:groups, :], dst_f[0:groups, :], AX.X, ALU.min).then_inc(prep, 1)
            dve.tensor_reduce(g_max[0:groups, :], dst_f[0:groups, :], AX.X, ALU.max).then_inc(prep, 1)
            dve.wait_ge(prep, 4)
            dve.tensor_scalar(rel_f[0:groups, :], dst_f[0:groups, :], g_min[0:groups, :], None,
                              ALU.subtract).then_inc(prep, 1)
            dve.wait_ge(counted, 3)
            dve.tensor_copy(iota[:, :], iota_i[:, :]).then_inc(counted, 1)
            dve.tensor_copy(first[:, :], first_i[:, :]).then_inc(counted, 1)
            dve.tensor_copy(need_f[:, 0:SLOTS * (early + 1)], need_i[:, 0:SLOTS * (early + 1)]).then_inc(counted, 1)
            n = CHUNKS
            for to in (rel_t, wgt_t, dst_t):
                for c in range(CHUNKS):
                    dve.wait_ge(turned, n + 1)
                    dve.tensor_copy(to[:, :, c], ps[n % 3][:, 0:groups]).then_inc(evacuated, 1)
                    n += 1
            dve.wait_ge(turned, n + 2)
            dve.tensor_copy(base_i[:, 0:groups], ps_r[0:1, 0:groups]).then_inc(prep, 1)
            dve.tensor_copy(base_f[:, 0:groups], ps_r[0:1, 0:groups]).then_inc(prep, 1)
            dve.wait_ge(prep, 7)
            dve.wait_ge(counted, 6)
            dve.tensor_tensor(span_row[:, 0:groups], ps_r[0:1, P:P + groups], base_f[:, 0:groups],
                              ALU.subtract).then_inc(prep, 1)
            checked = groups - first_checked
            dve.tensor_tensor(room_row[:, 0:checked], base_f[:, first_checked:groups], need_f[:, 0:checked],
                              ALU.subtract).then_inc(prep, 1)
            dve.wait_ge(prep, 9)
            dve.tensor_reduce(worst[:, 0:1], span_row[:, 0:groups], AX.X, ALU.max).then_inc(prep, 1)
            dve.tensor_reduce(worst[:, 1:2], room_row[:, 0:checked], AX.X, ALU.min).then_inc(prep, 1)
            dve.wait_ge(prep, 11)
            dve.tensor_scalar(worst[:, 2:3], worst[:, 0:1], float(WIN), None, ALU.is_lt).then_inc(prep, 1)
            dve.wait_ge(prep, 12)
            dve.tensor_scalar(regular[:, :], worst[:, 1:2], 0.0, worst[:, 2:3], ALU.is_ge,
                              ALU.mult).then_inc(prep, 1)
            dve.wait_ge(turned, n + 4)
            dve.tensor_copy(gb[:, :], ps_sum[0][:, 0:2 * dim]).then_inc(prep, 1)
            dve.tensor_copy(b1_all[:, :, :].rearrange("p e f -> p (e f)"),
                            ps_sum[1][:, 0:experts * FB]).then_inc(prep, 1)
            for k in range(KD):
                dve.memset(agg_t[:, k, :], 0.0).then_inc(prep, 1)
            dve.wait_ge(prep, PREP_ALL)

            def build(i, s, first):
                g = SLOTS * i + s
                if not (first and s < SUM_GAP):
                    dve.wait_ge(summed, g - SUM_GAP + 1)
                dve.tensor_tensor(onehot[:, s % SUM_BANKS, :, :], iota[:, :].unsqueeze(1).to_broadcast([P, CHUNKS, WIN]),
                                  rel_t[:, bass.ds(g, 1), :].rearrange("p a c -> p (a c)").unsqueeze(2).to_broadcast(
                                      [P, CHUNKS, WIN]), ALU.is_equal).then_inc(built, 1)

            def low_rows(i, s):
                g = SLOTS * i + s
                dve.wait_ge(x_high, g + 1)
                at = bass.ds(g, 1)
                for c in range(CHUNKS):
                    lo = dve.scalar_tensor_tensor(out=x_l[:, s % SUM_BANKS, c, :], in0=raw[:, s, c, :],
                                                  scalar=wgt_t[:, at, c:c + 1].rearrange("p a c -> p (a c)"),
                                                  in1=x_h[:, s % SUM_BANKS, c, :].bitcast(F32), op0=ALU.mult, op1=ALU.subtract)
                lo.then_inc(x_low, 1)
                dve.wait_ge(x_low, g + 1)
                dve.sem_inc(passed, 1)
                dve.tensor_copy(idx_slot[:, s, :], idx_t[:, bass.ds(g + SLOTS, 1), :].rearrange("p a c -> p (a c)")
                                ).then_inc(slot_ready, 1)

            def add_sums(g, s):
                dve.wait_ge(summed, g + 1)
                base = dve.value_load(base_i[0:1, bass.ds(g, 1)], min_val=0, max_val=nodes - 1)
                if not (isinstance(g, int) and g == 0):
                    dve.wait_ge(added, g)
                window = agg_t[:, :, bass.ds(base, WIN)]
                dve.tensor_tensor(window, window,
                                  ps_sum[s % SUM_BANKS][:, 0:KD * WIN].rearrange("p (k w) -> p k w", k=KD),
                                  ALU.add).then_inc(added, 1)

            def make_x1(k, n, b):
                at = x_sb[:, bass.ds(2 * k, n), :]
                dve.wait_ge(projected, k + 1)
                dve.tensor_tensor(at, at, ps_project[b][:, 0:n * dim].rearrange("p (t d) -> p t d", t=n),
                                  ALU.add).then_inc(x1_made, 1)
                dve.wait_ge(x1_made, k + 1)
                dve.sem_inc(passed, 1)
                for t in range(n):
                    bn = dve.bn_stats(t_stats[:, b, t, :],
                                      x_sb[:, bass.ds(2 * k + t, 1), :].rearrange("p a d -> p (a d)"))
                bn.then_inc(t_stat, 1)
                dve.wait_ge(t_stat, 2 * k + 1)
                dve.sem_inc(passed, 1)
                for t in range(n):
                    bn = dve.bn_aggr(t_mv[:, b, t, :], t_stats[:, b, t, :])
                bn.then_inc(t_stat, 1)

            def scale_pair(k, n, b):
                at = bass.ds(2 * k, n)
                dve.wait_ge(t_rooted, k + 1)
                dve.reciprocal(z_rstd[:, at], t_dev[:, b, 0:n]).then_inc(t_scaled, 1)
                dve.wait_ge(t_scaled, 2 * k + 1)
                dve.scalar_tensor_tensor(out=z_shift[:, at], in0=t_mv[:, b, 0:n, 0], scalar=-1.0,
                                         in1=z_rstd[:, at], op0=ALU.mult, op1=ALU.mult).then_inc(t_scaled, 1)

            def low_pair(k, n, b):
                dve.wait_ge(z_high, k + 1)
                at = bass.ds(2 * P * k, n * P)
                dve.tensor_tensor(zt_l[:, :, at], ps_turn[b][:, 0:KD * n * P].rearrange("p (k n) -> p k n", k=KD),
                                  zt_h[:, :, at].bitcast(F32), ALU.subtract).then_inc(z_low, 1)

            for s in range(SLOTS):
                build(0, s, True)
                low_rows(0, s)
                if s >= LAG:
                    add_sums(s - LAG, s - LAG)

            def dve_step(i, s):
                build(i, s, False)
                low_rows(i, s)
                add_sums(SLOTS * i + s - LAG, (s - LAG) % SLOTS)

            def last_sums():
                for g in range(groups - LAG, groups):
                    add_sums(g, g % SLOTS)

            with dve.Fori(1, FUSE) as i:
                for s in range(SLOTS):
                    dve_step(i, s)
            flag = dve.value_load(regular[0:1, 0:1])
            def dve_fused(i, first):
                for s in range(SLOTS):
                    dve_step(i, s)
                    if s == 2 and not first:
                        low_pair(i - FUSE - 1, 2, 0)
                    if s == 4:
                        make_x1(i - FUSE, 2, 0)
                    if s == 5:
                        scale_pair(i - FUSE, 2, 0)

            with dve.If(flag > 0):
                dve_fused(FUSE, True)
                with dve.Fori(FUSE + 1, rounds) as i:
                    dve_fused(i, False)
                last_sums()
                low_pair(early - 1, 2, 0)
            with dve.Else():
                with dve.Fori(FUSE, rounds) as i:
                    for s in range(SLOTS):
                        dve_step(i, s)
                last_sums()
                with dve.Fori(0, groups) as g:
                    gat = bass.ds(g, 1)
                    rel_g = rel_t[:, gat, :].rearrange("p a c -> p (a c)")
                    dst_g = dst_t[:, gat, :].rearrange("p a c -> p (a c)")
                    dve.tensor_scalar(g_key[:, :], rel_g, float(WIN), None, ALU.is_ge).then_inc(gen_key, 1)
                    dve.wait_ge(gen_key, 3 * g + 1)
                    dve.scalar_tensor_tensor(out=g_key[:, :], in0=dst_g, scalar=1.0, in1=g_key[:, :],
                                             op0=ALU.add, op1=ALU.mult).then_inc(gen_key, 1)
                    dve.wait_ge(gen_key, 3 * g + 2)
                    dve.tensor_scalar(g_key[:, :], g_key[:, :], -1.0, None, ALU.add).then_inc(gen_key, 1)
                    dve.wait_ge(gen_key, 3 * g + 3)
                    for c in range(CHUNKS):
                        done = CHUNKS * g + c
                        dve.wait_ge(gen_high, done + 1)
                        dve.sem_inc(passed, 1)
                        dve.scalar_tensor_tensor(out=x_l[:, 0, 0, :], in0=raw[:, 0, 0, :],
                                                 scalar=wgt_t[:, gat, c:c + 1].rearrange("p a c -> p (a c)"),
                                                 in1=x_h[:, 0, 0, :].bitcast(F32), op0=ALU.mult,
                                                 op1=ALU.subtract).then_inc(gen_low, 1)
                        with dve.Fori(0, windows) as v:
                            step = windows * done + v
                            dve.tensor_scalar(g_hit[:, 0:1], g_key[:, c:c + 1], first[:, bass.ds(v, 1)], None,
                                              ALU.subtract).then_inc(gen_win, 1)
                            dve.wait_ge(gen_win, step + 1)
                            dve.tensor_scalar(onehot[:, 0, 0, :], iota[:, :], g_hit[:, 0:1], None,
                                              ALU.is_equal).then_inc(gen_hot, 1)
                            dve.wait_ge(gen_mm, step + 2)
                            window = agg_t[:, :, bass.ds(WIN * v, WIN)]
                            dve.tensor_tensor(window, window,
                                              ps_sum[0][:, 0:KD * WIN].rearrange("p (k w) -> p k w", k=KD),
                                              ALU.add).then_inc(gen_add, 1)
                            dve.wait_ge(gen_add, step + 1)
                dve.sem_inc(gen_done, 1)
                with dve.Fori(0, early) as k:
                    make_x1(k, 2, 0)
                    scale_pair(k, 2, 0)
                    low_pair(k, 2, 0)
            q, r = late
            for stage, pair in ((make_x1, q), (scale_pair, q), (make_x1, r), (scale_pair, r), (low_pair, q)):
                stage(*pair)

            count = [0]

            def step(ins):
                count[0] += 1
                ins.then_inc(route_v, 1)
                dve.wait_ge(route_v, count[0])

            dve.wait_ge(z_counted, pairs + 1)
            step(dve.tensor_scalar(col_mean[:, :], ps_r[:, 0:KD], 1.0 / nodes, None, ALU.mult))
            assert count[0] == ROUTE_COLS
            low_pair(*r)
            dve.wait_ge(route_p, 1)
            step(dve.tensor_tensor(logit[:, :], ps_r[0:1, 8:8 + experts], br_sb[:, :], ALU.add))
            step(dve.tensor_reduce(r_s[:, 0:1], logit[:, :], AX.X, ALU.max))
            step(dve.tensor_scalar(logit[:, :], logit[:, :], r_s[:, 0:1], None, ALU.subtract))
            assert count[0] == ROUTE_MAX0
            dve.wait_ge(route_a, 1)
            step(dve.reciprocal(r_s[:, 1:2], r_s[:, 1:2]))
            step(dve.tensor_scalar(r_w[:, :], r_exp[:, :], r_s[:, 1:2], None, ALU.mult))
            step(dve.tensor_scalar(r_scale[:, :], r_w[:, :], float(nodes), None, ALU.mult))
            step(dve.reciprocal(r_scale[:, :], r_scale[:, :]))
            step(dve.tensor_scalar(r_scale[:, :], r_scale[:, :], capacity, 1.0, ALU.mult, ALU.min))
            step(dve.tensor_tensor(r_w[:, :], r_w[:, :], r_scale[:, :], ALU.mult))
            step(dve.tensor_reduce(r_s[:, 2:3], r_w[:, :], AX.X, ALU.max))
            step(dve.tensor_scalar(r_w[:, :], r_w[:, :], r_s[:, 2:3], None, ALU.subtract))
            assert count[0] == ROUTE_MAX1
            dve.wait_ge(route_a, 2)
            step(dve.reciprocal(r_s[:, 3:4], r_s[:, 3:4]))
            step(dve.tensor_scalar(r_w[:, :], r_exp[:, :], r_s[:, 3:4], None, ALU.mult))
            step(dve.max(top_v[:, :], r_w[:, :]))
            step(dve.max_index(top_i[:, :], top_v[:, :], r_w[:, :]))
            assert count[0] == ROUTE_TOP
            step(dve.tensor_scalar(r_s[:, 6:8], top_v[:, 0:2], top_v[:, 0:1], None, ALU.subtract))
            assert count[0] == ROUTE_PAIR
            step(dve.tensor_copy(top_if[:, :], top_i[:, :]))
            dve.wait_ge(route_a, 3)
            step(dve.reciprocal(r_s[:, 5:6], r_s[:, 5:6]))
            step(dve.tensor_scalar(top_w[:, :], top_w[:, :], r_s[:, 5:6], None, ALU.mult))
            for e in range(2):
                step(dve.tensor_scalar(dense[:, e, :], iota[0:1, 0:experts], top_if[:, e:e + 1], top_w[:, e:e + 1],
                                       ALU.is_equal, ALU.mult))
            step(dve.tensor_tensor(dense[:, 0, :], dense[:, 0, :], dense[:, 1, :], ALU.add))
            assert count[0] == ROUTE_DENSE
            dve.wait_ge(route_p, 3)
            step(dve.tensor_copy(top_wb[:, :], ps_r[:, 16:18]))
            step(dve.tensor_copy(dense_b[:, :], ps_r[0:experts, P:2 * P]))
            dve.wait_ge(route_p, 4)
            step(dve.tensor_copy(bias_b[:, :], ps_r[:, 256:256 + dim]))
            assert count[0] == ROUTE_BIAS

            def make_res(q, b):
                if not (isinstance(q, int) and q < 2):
                    dve.wait_ge(o_made, SPAN_TILES * (q - 1))
                    dve.sem_inc(passed, 1)
                for t in range(SPAN_TILES):
                    at = bass.ds(SPAN_TILES * q + t, 1)
                    r = dve.tensor_scalar(res[:, b, t, :], x_sb[:, at, :].rearrange("p a d -> p (a d)"),
                                          z_rstd[:, at], z_shift[:, at], ALU.mult, ALU.add)
                r.then_inc(res_made, 1)

            def low_block(q, b, m, cols):
                dve.wait_ge(gelu_done, HB * q + m + 1)
                dve.tensor_tensor(h_l[:, b, m, 0:cols], h_x[:, m % 2, 0:cols], h_h[:, b, m, 0:cols].bitcast(F32),
                                  ALU.subtract).then_inc(h_low, 1)

            def sum_tile(q, b, j, reused=True):
                if j == 0:
                    dve.wait_ge(res_biased, q + 1)
                    if reused:
                        dve.wait_ge(y_gamma, q)
                dve.wait_ge(l2_done, SPAN_TILES * q + j + 1)
                dve.tensor_tensor(o_t[:, b, j, :], res[:, b, j, :],
                                  ps_sum[(SPAN_TILES * b + j) % SUM_BANKS][:, 0:dim], ALU.add).then_inc(o_made, 1)

            def newton(q, k, ins):
                ins.then_inc(root, 1)
                dve.wait_ge(root, NEWTON_STEPS * q + k + 1)

            def norm_part(q, b, n, part):
                v, y, e = f_var[:, 0:n], f_root[:, 0:n], f_corr[:, 0:n]
                if part == 0:
                    dve.wait_ge(o_made, SPAN_TILES * q + n)
                    dve.sem_inc(passed, 1)
                    for j in range(n):
                        bn = dve.bn_stats(f_stats[:, j, :], o_t[:, b, j, :])
                    bn.then_inc(o_stat, 1)
                if part == 1:
                    dve.wait_ge(o_stat, 2 * q + 1)
                    dve.sem_inc(passed, 1)
                    for j in range(n):
                        bn = dve.bn_aggr(f_mv[:, j, :], f_stats[:, j, :])
                    bn.then_inc(o_stat, 1)
                if part == 2:
                    dve.wait_ge(o_stat, 2 * q + 2)
                    newton(q, 0, dve.tensor_scalar(v, f_mv[:, 0:n, 1], EPS, None, ALU.add))
                    newton(q, 1, dve.tensor_scalar(y.bitcast(I32), v.bitcast(I32), 1, None, ALU.logical_shift_right))
                    newton(q, 2, dve.tensor_scalar(y.bitcast(I32), y.bitcast(I32), -1.0, ROOT_MAGIC,
                                                   ALU.mult, ALU.add))
                if 3 <= part < 3 + NEWTON:
                    k = 3 + 4 * (part - 3)
                    newton(q, k, dve.tensor_tensor(e, y, y, ALU.mult))
                    newton(q, k + 1, dve.tensor_tensor(e, e, v, ALU.mult))
                    newton(q, k + 2, dve.tensor_scalar(e, e, -0.5, 1.5, ALU.mult, ALU.add))
                    newton(q, k + 3, dve.tensor_tensor(y, y, e, ALU.mult))
                if part == 6:
                    dve.scalar_tensor_tensor(out=f_shift[:, 0:n], in0=f_mv[:, 0:n, 0], scalar=-1.0, in1=y,
                                             op0=ALU.mult, op1=ALU.mult).then_inc(f_shifted, 1)
                if part == 7:
                    dve.wait_ge(f_shifted, q + 1)
                    for j in range(n):
                        o = dve.tensor_scalar(o_t[:, b, j, :], o_t[:, b, j, :], f_root[:, j:j + 1],
                                              f_shift[:, j:j + 1], ALU.mult, ALU.add)
                    o.then_inc(o_normed, 1)

            for e in range(2):
                dve.wait_ge(w1_high, e + 1)
                dve.tensor_tensor(w1_l[:, e, :, :], w1_raw[:, e, :, :], w1_h[:, e, :, :].bitcast(F32),
                                  ALU.subtract).then_inc(w1_low, 1)
            for e in range(2):
                dve.wait_ge(w2_in[e], 16)
                dve.tensor_scalar(w2_raw[:, e, :, :], w2_raw[:, e, :, :], top_wb[:, e:e + 1], None,
                                  ALU.mult).then_inc(w2_scaled, 1)
            make_res(0, 0)
            make_res(1, 1)
            for m in range(HB):
                low_block(0, 0, m, SPAN)
            for e in range(2):
                dve.wait_ge(w2_high, e + 1)
                dve.tensor_tensor(w2_l[:, e, :, :], w2_raw[:, e, :, :], w2_h[:, e, :, :].bitcast(F32),
                                  ALU.subtract).then_inc(w2_low, 1)
            for m in range(HB):
                low_block(1, 1, m, SPAN)
                if m in SUM_AFTER:
                    sum_tile(0, 0, SUM_AFTER.index(m), reused=False)
            make_res(2, 0)
            with dve.Fori(1, spans // 2) as i:
                for b in (1, 0):
                    q = 2 * i - b
                    for m in range(HB):
                        low_block(q + 1, 1 - b, m, SPAN)
                        norm_part(q - 1, 1 - b, SPAN_TILES, m)
                        if m in SUM_AFTER:
                            sum_tile(q, b, SUM_AFTER.index(m))
                    make_res(q + 2, b)
            for m in range(HB):
                low_block(spans, 0, m, P)
                norm_part(spans - 2, 0, SPAN_TILES, m)
                if m in SUM_AFTER:
                    sum_tile(spans - 1, 1, SUM_AFTER.index(m))

            def finish_last(y, q, b, n):
                dve.wait_ge(o_normed, q + 1)
                dve.tensor_tensor(y, o_t[:, b, 0:n, :], gb[:, 0:dim].unsqueeze(1).to_broadcast([P, n, dim]),
                                  ALU.mult).then_inc(last_gamma, 1)
                dve.wait_ge(last_gamma, q - spans + 2)
                dve.wait_ge(x1_beta, q + 1)
                dve.tensor_tensor(y, y, x_sb[:, SPAN_TILES * q:SPAN_TILES * q + n, :],
                                  ALU.add).then_inc(last_made, 1)

            for m in range(HB):
                norm_part(spans - 1, 1, SPAN_TILES, m)
            dve.wait_ge(stored[1], 16 * (spans // 2 - 1))
            finish_last(y_out[:, 1, :, :], spans - 1, 1, SPAN_TILES)
            sum_tile(spans, 0, 0)
            for m in range(HB):
                norm_part(spans, 0, 1, m)
            finish_last(y_last[:, :].unsqueeze(1), spans, 0, 1)


_INS = ["x", "src", "dst", "edge_weight", "L0_gnn_weight", "L0_ffn_Wr", "L0_ffn_br", "L0_ffn_W1", "L0_ffn_b1",
        "L0_ffn_W2", "L0_ffn_b2", "L0_ffn_gamma", "L0_ffn_beta"]


def kernel(**inputs):
    import numpy as _np
    import concourse.bacc as _bacc
    from concourse import mybir as _mybir
    from concourse.bass_utils import run_bass_kernel_spmd as _run

    nc = _bacc.Bacc("TRN2", target_bir_lowering=False, num_devices=1)
    arrays, args = {}, []
    for name in _INS:
        a = _np.ascontiguousarray(inputs[name])
        arrays[f"in_{name}_dram"] = a
        args.append(nc.dram_tensor(f"in_{name}_dram", a.shape, _mybir.dt.from_np(a.dtype), kind="ExternalInput").ap())
    out = nc.dram_tensor("out_0_dram", inputs["x"].shape, _mybir.dt.float32, kind="ExternalOutput").ap()
    table = nc.dram_tensor("table", inputs["x"].shape, _mybir.dt.float32).ap()
    gnn_moe(nc, *args, table, out)
    r = _run(nc, [arrays], core_ids=[0])
    return r.results[0]["out_0_dram"]
```

```python
import math
from contextlib import ExitStack

import concourse.bass as bass
from concourse import mybir

ALU = mybir.AluOpType
ACT = mybir.ActivationFunctionType
AX = mybir.AxisListType
F32 = mybir.dt.float32
F32R = mybir.dt.float32r
I32 = mybir.dt.int32
U32 = mybir.dt.uint32

P = 128
EPS = 1e-5
CHUNKS = 4
GROUP = CHUNKS * P
WIN = 40
SLOTS = 7
SUM_BANKS = 4
SUM_GAP = 3
LAG = 3
RAW_GROUPS = 5
FUSE = 3
FUSE_SLOT = 2
SPAN_TILES = 3
HALVES = 2
W2_AFTER = (3, 5)
TILE_AFTER = (2, 5, 7)
SUM_AFTER = (3, 6, 7)
CAPACITY_FACTOR = 1.25

PREP_SRC, PREP_DST, PREP_REL, PREP_FLAG = 1, 2, 5, 13
ROUTE_COLS, ROUTE_MAX0, ROUTE_MAX1, ROUTE_TOP, ROUTE_PAIR, ROUTE_DENSE, ROUTE_BIAS = 1, 4, 11, 15, 16, 22, 25
TURNED_WGT, TURNED_DST, TURNED_REL, TURNED_ALL = 4, 10, 14, 20
ROOT_MAGIC = float(0x5F3759DF)
NEWTON = 3
NEWTON_STEPS = 3 + 4 * NEWTON


def gnn_moe(nc, x, src, dst, edge_weight, gnn_w, wr, br, w1, b1, w2, b2, gamma, beta, table, out):
    nodes, dim = x.shape
    edges = src.shape[0]
    experts, _, hidden = w1.shape
    KD = dim // P
    FB = hidden // P
    HB = 2 * FB
    groups = -(-edges // GROUP)
    full = edges // GROUP
    rest = edges - full * GROUP
    last_chunks = -(-rest // P)
    even = full // 16 * 16
    rounds = groups // SLOTS
    assert groups == rounds * SLOTS and groups == full + 1 and groups <= P
    tiles = -(-nodes // P)
    tail = nodes - (tiles - 1) * P
    batches = [(0, 5), (tiles - 6, tiles), (5, 10), (10, 15), (15, tiles - 6)]
    by_dve = (0, 0, 0, 2, 3)
    with_tail = 1
    width = tiles * P
    assert nodes - 1 + WIN <= width
    windows = width // WIN
    pairs = tiles // 2
    early = rounds - FUSE
    late = [(k, min(2, tiles - 2 * k), (k - early + 1) % 2) for k in range(early, pairs + 1)]
    assert len(late) == 2 and tiles == 2 * pairs + 1
    first_checked = SLOTS * FUSE + FUSE_SLOT - LAG
    assert first_checked + SLOTS * early == groups - 1
    SPAN = SPAN_TILES * P
    spans = tiles // SPAN_TILES
    assert tiles == spans * SPAN_TILES + 1 and spans % 2 == 0
    tiles_up = (spans + 1) * SPAN_TILES
    LAST = ((1, 0, SPAN_TILES), (0, SPAN_TILES, SPAN_TILES + 1))
    capacity = float(math.ceil(nodes * CAPACITY_FACTOR / experts))

    def chunks_of(i, s):
        return last_chunks if isinstance(i, int) and SLOTS * i + s == groups - 1 else CHUNKS

    with ExitStack() as ctx:
        def sb(name, shape, dt=F32):
            return ctx.enter_context(nc.sbuf_tensor(name, shape, dt))

        def sem(name):
            return ctx.enter_context(nc.semaphore(name))

        agg_t = sb("agg_t", [P, KD, width])
        x_sb = sb("x_sb", [P, tiles_up, dim])
        zt_h = sb("zt_h", [P, KD, width], F32R)
        zt_l = sb("zt_l", [P, KD, width], F32R)
        z_rstd = sb("z_rstd", [P, tiles_up])
        z_shift = sb("z_shift", [P, tiles_up])
        ident = sb("ident", [P, P])
        regular = sb("regular", [1, 1], I32)
        iota = sb("iota", [P, WIN])
        ones = sb("ones", [1, P])
        eps = sb("eps", [P, 1])
        zero = sb("zero", [P, 1])
        b1_all = sb("b1_all", [P, experts, FB])
        b2_sb = sb("b2_sb", [experts, dim])
        wr_sb = sb("wr_sb", [P, KD, experts])
        br_sb = sb("br_sb", [1, experts])
        gb = sb("gb", [P, 2 * dim])
        bias_b = sb("bias_b", [P, dim])
        z_sums = sb("z_sums", [P, KD, pairs + 1])
        col_sum = sb("col_sum", [P, KD])
        logit = sb("logit", [1, experts])
        r_exp = sb("r_exp", [1, experts])
        r_w = sb("r_w", [1, experts])
        r_scale = sb("r_scale", [1, experts])
        r_s = sb("r_s", [1, 8])
        top_v = sb("top_v", [1, 8])
        top_i = sb("top_i", [1, 8], U32)
        top_if = sb("top_if", [1, 8])
        top_w = sb("top_w", [1, 2])
        dense = sb("dense", [1, 2, experts])
        dense_b = sb("dense_b", [experts, P])
        top_wb = sb("top_wb", [P, 2])
        b1_s = sb("b1_s", [P, 2, FB])
        spare = sb("spare", [1, 3])
        f_stats = sb("f_stats", [P, SPAN_TILES, 6])
        f_mv = sb("f_mv", [P, SPAN_TILES, 2])
        f_var = sb("f_var", [P, SPAN_TILES])
        f_root = sb("f_root", [P, SPAN_TILES])
        f_corr = sb("f_corr", [P, SPAN_TILES])
        f_shift = sb("f_shift", [P, SPAN_TILES])
        last_stats = sb("last_stats", [P, SPAN_TILES + 1, 6])
        last_mv = sb("last_mv", [P, SPAN_TILES + 1, 2])
        last_dev = sb("last_dev", [P, SPAN_TILES + 1])
        last_rstd = sb("last_rstd", [P, SPAN_TILES + 1])
        last_shift = sb("last_shift", [P, SPAN_TILES + 1])

        with ExitStack() as early_ctx:
            def sb1(name, shape, dt=F32):
                return early_ctx.enter_context(nc.sbuf_tensor(name, shape, dt))

            g_min = sb1("g_min", [P, 1])
            g_max = sb1("g_max", [P, 1])
            base_i = sb1("base_i", [1, P], I32)
            base_f = sb1("base_f", [1, P])
            need_i = sb1("need_i", [1, P], I32)
            need_f = sb1("need_f", [1, P])
            span_row = sb1("span_row", [1, P])
            room_row = sb1("room_row", [1, P])
            worst = sb1("worst", [1, 3])
            idx_t = sb1("idx_t", [P, groups + SLOTS, CHUNKS], I32)
            rel_t = sb1("rel_t", [P, groups, CHUNKS])
            wgt_t = sb1("wgt_t", [P, groups, CHUNKS])
            dst_t = sb1("dst_t", [P, groups, CHUNKS])
            idx_slot = sb1("idx_slot", [P, SLOTS, CHUNKS], I32)
            raw = sb1("raw", [P, SLOTS, CHUNKS, dim])
            with ExitStack() as table_ctx:
                xn = table_ctx.enter_context(nc.sbuf_tensor("xn", [P, tiles, dim], F32))
            x_h = sb1("x_h", [P, SUM_BANKS, CHUNKS, dim], F32R)
            x_l = sb1("x_l", [P, SUM_BANKS, CHUNKS, dim], F32R)
            assert 6 * GROUP <= width
            prepare = agg_t[:, :, :].rearrange("p k n -> p (k n)")[:, 0:6 * GROUP].rearrange("p (n e) -> p n e", n=6)
            src_rows, dst_rows = (prepare[:, n, :].bitcast(I32) for n in range(2))
            wgt_rows, src_f, dst_f = (prepare[:, n, :] for n in range(2, 5))
            rel_f = prepare[:, 5, :]
            onehot = sb1("onehot", [P, SUM_BANKS, CHUNKS, WIN], F32R)
            n_stats = sb1("n_stats", [P, tiles, 6])
            n_mv = sb1("n_mv", [P, tiles, 2])
            n_dev = sb1("n_dev", [P, tiles])
            n_rstd = sb1("n_rstd", [P, tiles])
            n_shift = sb1("n_shift", [P, tiles])
            r_stats = sb1("r_stats", [P, RAW_GROUPS, CHUNKS, 6])
            r_mv = sb1("r_mv", [P, RAW_GROUPS, CHUNKS, 2])
            r_dev = sb1("r_dev", [P, RAW_GROUPS, CHUNKS])
            r_rstd = sb1("r_rstd", [P, RAW_GROUPS, CHUNKS])
            r_shift = sb1("r_shift", [P, RAW_GROUPS, CHUNKS])
            iota_i = sb1("iota_i", [P, WIN], I32)
            first_i = sb1("first_i", [P, windows], I32)
            first = sb1("first", [P, windows])
            g_key = sb1("g_key", [P, CHUNKS])
            g_idx = sb1("g_idx", [P, 1], I32)
            g_hit = sb1("g_hit", [P, 1])
            gw_sb = sb1("gw_sb", [P, KD, dim])
            gb_row = sb1("gb_row", [1, 2 * dim])
            b1_rows = sb1("b1_rows", [experts * FB, P])
            agg_pair = sb1("agg_pair", [P, 2, KD, 2 * P])
            z_pair = sb1("z_pair", [P, 2, 2, dim])
            t_stats = sb1("t_stats", [P, 2, 2, 6])
            t_mv = sb1("t_mv", [P, 2, 2, 2])
            t_dev = sb1("t_dev", [P, 2, 2])

        w1_h = sb("w1_h", [P, 2, KD, hidden], F32R)
        w1_l = sb("w1_l", [P, 2, KD, hidden], F32R)
        w2_h = sb("w2_h", [P, 2, FB, dim], F32R)
        w2_l = sb("w2_l", [P, 2, FB, dim], F32R)
        h_h = sb("h_h", [P, 2, HB, SPAN], F32R)
        h_l = sb("h_l", [P, 2, HB, SPAN], F32R)
        h_x = sb("h_x", [P, 2, SPAN])
        y_out = sb("y_out", [P, 2, SPAN_TILES, dim])
        y_last = sb("y_last", [P, dim])
        flat = agg_t[:, :, :].rearrange("p k n -> p (k n)")
        W1N, W2N, RN = 2 * KD * hidden, 2 * FB * dim, 2 * SPAN_TILES * dim
        w1_raw = flat[:, 0:W1N].rearrange("p (e k f) -> p e k f", e=2, k=KD)
        w2_raw = flat[:, W1N:W1N + W2N].rearrange("p (e f d) -> p e f d", e=2, f=FB)
        res = flat[:, W1N + W2N:W1N + W2N + RN].rearrange("p (b t d) -> p b t d", b=2, t=SPAN_TILES)
        o_t = flat[:, 0:RN].rearrange("p (b t d) -> p b t d", b=2, t=SPAN_TILES)

        ps = [ctx.enter_context(nc.psum_tensor(f"ps{i}", [P, 512], F32)) for i in range(3)]
        ps_sum = [ctx.enter_context(nc.psum_tensor(f"ps_sum{i}", [P, 512], F32)) for i in range(SUM_BANKS)]
        ps_r = ctx.enter_context(nc.psum_tensor("ps_r", [P, 512], F32))
        ps_project = [ps[0], ps[2]]

        def ps_turn(k, b):
            return ps_sum[1] if isinstance(k, int) and k == pairs else (ps[1], ps_sum[0])[b]

        ps_hidden = ps + [ps_r]

        src_in, dst_in, wgt_in, gw_in, small_in, router_in = (sem(n) for n in (
            "src_in", "dst_in", "wgt_in", "gw_in", "small_in", "router_in"))
        x_in = [sem(f"x_in{j}") for j in range(len(batches))]
        n_stat = sem("n_stat")
        n_rooted = sem("n_rooted")
        n_scaled = sem("n_scaled")
        r_stat, r_rooted, r_scaled, r_normed = (sem(n) for n in ("r_stat", "r_rooted", "r_scaled", "r_normed"))
        cleared = sem("cleared")
        n_act, n_dve = sem("n_act"), sem("n_dve")
        table_in = sem("table_in")
        w1_in = [sem(f"w1_in{n}") for n in range(2 * HALVES)]
        w2_in = [sem("w2_in0"), sem("w2_in1")]
        zeroed = sem("zeroed")
        counted = sem("counted")
        constants = sem("constants")
        ident_set = sem("ident_set")
        prep = sem("prep")
        turned = sem("turned")
        evac_v, evac_a = sem("evac_v"), sem("evac_a")
        spread = sem("spread")
        gathered = [sem(f"gathered{s}") for s in range(SLOTS)]
        slot_ready = sem("slot_ready")
        passed = sem("passed")
        built = sem("built")
        x_high = sem("x_high")
        x_low = sem("x_low")
        summed = sem("summed")
        added = sem("added")
        gen_gather, gen_high, gen_low = sem("gen_gather"), sem("gen_high"), sem("gen_low")
        gen_idx, gen_hot, gen_mm, gen_add = sem("gen_idx"), sem("gen_hot"), sem("gen_mm"), sem("gen_add")
        gen_key, gen_win, gen_done = sem("gen_key"), sem("gen_win"), sem("gen_done")
        copied = sem("copied")
        projected = sem("projected")
        x1_made = sem("x1_made")
        t_stat = sem("t_stat")
        t_rooted = sem("t_rooted")
        t_scaled = sem("t_scaled")
        z_made = sem("z_made")
        z_turned = sem("z_turned")
        z_high = sem("z_high")
        z_low = sem("z_low")
        z_counted = sem("z_counted")
        route_v, route_a, route_p = sem("route_v"), sem("route_a"), sem("route_p")
        b1_picked = sem("b1_picked")
        w1_high, w1_low, w2_high, w2_low = (sem(n) for n in ("w1_high", "w1_low", "w2_high", "w2_low"))
        l1_done = sem("l1_done")
        gelu_done = sem("gelu_done")
        h_low = sem("h_low")
        l2_done = sem("l2_done")
        res_made = sem("res_made")
        res_biased = sem("res_biased")
        o_made = sem("o_made")
        o_stat = sem("o_stat")
        f_shifted = sem("f_shifted")
        root = sem("root")
        o_normed = sem("o_normed")
        x1_beta = sem("x1_beta")
        y_gamma, y_made = sem("y_gamma"), sem("y_made")
        last_stat, last_rooted, last_scaled, last_normed = (sem(n) for n in (
            "last_stat", "last_rooted", "last_scaled", "last_normed"))
        last_gamma, last_made = sem("last_gamma"), sem("last_made")
        stored = [sem("stored0"), sem("stored1")]

        block = ctx.enter_context(nc.Block())

        @block.sync
        def _(sp):
            def load_edges(to, of, done):
                by_group = of[0:full * GROUP].rearrange("(g e) -> g e", e=GROUP)
                sp.dma_start(to[0:even, :], by_group[0:even, :]).then_inc(done, 16)
                sp.dma_start(to[even:full, :], by_group[even:full, :]).then_inc(done, 16)
                sp.dma_start(to[full:groups, 0:rest],
                             of[full * GROUP:edges].rearrange("(a e) -> a e", a=1)).then_inc(done, 16)

            sp.wait_ge(zeroed, 1)
            load_edges(src_rows, src, src_in)
            for j, (lo, hi) in enumerate(batches):
                whole = min(hi, tiles - 1)
                sp.dma_start(x_sb[:, lo:whole, :],
                             x[lo * P:whole * P, :].rearrange("(t p) d -> p t d", p=P)).then_inc(x_in[j], 16)
                if j == with_tail:
                    sp.wait_ge(zeroed, 3)
                    sp.dma_start(x_sb[0:tail, tiles - 1, :], x[(tiles - 1) * P:nodes, :]).then_inc(x_in[j], 16)
            load_edges(dst_rows, dst, dst_in)
            sp.dma_start(dst_rows[full:groups, rest:GROUP],
                         dst[edges - (GROUP - rest):edges].rearrange("(a e) -> a e", a=1)).then_inc(dst_in, 16)
            load_edges(wgt_rows, edge_weight, wgt_in)
            sp.dma_start(gb_row[:, 0:dim], gamma.rearrange("(a n) -> a n", a=1)).then_inc(small_in, 16)
            sp.dma_start(gb_row[:, dim:2 * dim], beta.rearrange("(a n) -> a n", a=1)).then_inc(small_in, 16)
            sp.dma_start(b1_rows[:, :], b1.rearrange("e (f p) -> (e f) p", p=P)).then_inc(small_in, 16)
            for j, (lo, hi) in enumerate(batches):
                whole = min(hi, tiles - 1)
                sp.wait_ge(n_act, j + 1)
                if by_dve[j]:
                    sp.wait_ge(n_dve, sum(b > 0 for b in by_dve[:j + 1]))
                sp.dma_start(table[lo * P:whole * P, :].rearrange("(t p) d -> p t d", p=P),
                             xn[:, lo:whole, :]).then_inc(table_in, 16)
                if j == with_tail:
                    sp.dma_start(table[(tiles - 1) * P:nodes, :], xn[0:tail, tiles - 1, :]).then_inc(table_in, 16)
            sp.dma_start(wr_sb[:, :, :], wr.rearrange("(k p) n -> p k n", p=P)).then_inc(router_in, 16)
            sp.dma_start(br_sb[:, :], br.rearrange("(a n) -> a n", a=1)).then_inc(router_in, 16)
            sp.dma_start(b2_sb[:, :], b2).then_inc(router_in, 16)
            sp.dma_start(gw_sb[:, :, :], gnn_w.rearrange("(k p) n -> p k n", p=P)).then_inc(gw_in, 16)
            sp.wait_ge(route_v, ROUTE_TOP)
            which = [sp.value_load(top_i[0:1, e:e + 1], min_val=0, max_val=experts - 1) for e in range(2)]
            for e in range(2):
                for h in range(HALVES):
                    at = slice(h * hidden // HALVES, (h + 1) * hidden // HALVES)
                    sp.dma_start(w1_raw[:, e, :, at], w1[bass.ds(which[e], 1), :, at].rearrange(
                        "a (k p) f -> p (a k) f", p=P)).then_inc(w1_in[HALVES * e + h], 16)
            for e in range(2):
                sp.dma_start(w2_raw[:, e, :, :],
                             w2[bass.ds(which[e], 1)].rearrange("a (f p) d -> p (a f) d", p=P)).then_inc(w2_in[e], 16)
            def store(q, b):
                sp.dma_start(out[bass.ds(SPAN * q, SPAN), :].rearrange("(t p) d -> p t d", p=P),
                             y_out[:, b, :, :]).then_inc(stored[b], 16)

            with sp.Fori(0, spans // 2 - 1) as i:
                for b in range(2):
                    sp.wait_ge(y_made, 2 * i + b + 1)
                    store(2 * i + b, b)
            sp.wait_ge(y_made, spans - 1)
            store(spans - 2, 0)
            sp.wait_ge(last_made, 1)
            store(spans - 1, 1)
            sp.wait_ge(last_made, 2)
            sp.dma_start(out[spans * SPAN:nodes, :], y_last[0:tail, :]).then_inc(stored[0], 16)
            sp.wait_ge(stored[0], 16 * (spans // 2 + 1))
            sp.wait_ge(stored[1], 16 * (spans // 2))

        @block.gpsimd
        def _(pool):
            pool.memset(ident[:, :], 0.0).then_inc(ident_set, 1)
            pool.wait_ge(ident_set, 1)
            pool.affine_select(out=ident[:, :], in_=ident[:, :], compare_op=ALU.not_equal, fill=1.0, base=0,
                               pattern=[[-1, P]], channel_multiplier=1).then_inc(ident_set, 1)
            pool.iota(iota_i[:, :], pattern=[[1, WIN]], base=0, channel_multiplier=0).then_inc(counted, 1)
            pool.iota(first_i[:, :], pattern=[[WIN, windows]], base=0, channel_multiplier=0).then_inc(counted, 1)
            pool.iota(need_i[:, 0:SLOTS * (early + 1)], pattern=[[2 * P, early + 1], [0, SLOTS]], base=2 * P,
                      channel_multiplier=0).then_inc(counted, 1)

            pool.memset(agg_t[:, 1:KD, :], 0.0).then_inc(cleared, 1)

            def gather_group(i, s, rows=table):
                for c in range(chunks_of(i, s)):
                    pool.indirect_dma_start(
                        out=raw[:, s, c, :], out_offset=None, in_=rows,
                        in_offset=bass.IndirectOffsetOnAxis(ap=idx_slot[:, s, c:c + 1], axis=0),
                    ).then_inc(gathered[s], 16)

            for s in range(SLOTS):
                pool.wait_ge(slot_ready, s + 1)
                if s == RAW_GROUPS:
                    pool.wait_ge(table_in, 16 * (len(batches) + 1))
                gather_group(0, s, x if s < RAW_GROUPS else table)

            def gather_round(i):
                for s in range(SLOTS):
                    pool.wait_ge(slot_ready, SLOTS * i + s + 1)
                    pool.sem_inc(passed, 1)
                    gather_group(i, s)

            with pool.Fori(1, rounds - 1) as i:
                gather_round(i)
            gather_round(rounds - 1)

            pool.wait_ge(prep, PREP_FLAG)
            flag = pool.value_load(regular[0:1, 0:1])
            with pool.If(flag < 1):
                with pool.Fori(0, groups) as g:
                    for c in range(CHUNKS):
                        pool.wait_ge(gen_idx, CHUNKS * g + c + 1)
                        pool.sem_inc(passed, 1)
                        pool.indirect_dma_start(
                            out=raw[:, 0, 0, :], out_offset=None, in_=table,
                            in_offset=bass.IndirectOffsetOnAxis(ap=g_idx[:, 0:1], axis=0),
                        ).then_inc(gen_gather, 16)

            def over(a, n):
                return a.unsqueeze(1).to_broadcast([P, n, dim])

            def add_bias(q, b, n):
                pool.wait_ge(res_made, q + 1)
                pool.tensor_tensor(res[:, b, 0:n, :], res[:, b, 0:n, :], over(bias_b[:, :], n),
                                   ALU.add).then_inc(res_biased, 1)
                at = x_sb[:, SPAN_TILES * q:SPAN_TILES * q + n, :] if isinstance(q, int) else \
                    x_sb[:, bass.ds(SPAN_TILES * q, n), :]
                pool.tensor_tensor(at, at, over(gb[:, dim:2 * dim], n), ALU.add).then_inc(x1_beta, 1)

            def finish(q, b, n, stores):
                y, at = y_out[:, b, 0:n, :], x_sb[:, bass.ds(SPAN_TILES * q, n), :]
                if stores is not None:
                    pool.wait_ge(stored[b], stores)
                pool.wait_ge(o_normed, q + 1)
                pool.tensor_tensor(y, o_t[:, b, 0:n, :], over(gb[:, 0:dim], n), ALU.mult).then_inc(y_gamma, 1)
                pool.wait_ge(y_gamma, q + 2)
                pool.tensor_tensor(y, y, at, ALU.add).then_inc(y_made, 1)

            pool.wait_ge(route_v, ROUTE_BIAS)
            pool.sem_inc(y_gamma, 1)
            for q in range(3):
                add_bias(q, q % 2, SPAN_TILES)
            finish(0, 0, SPAN_TILES, None)
            add_bias(3, 1, SPAN_TILES)
            finish(1, 1, SPAN_TILES, None)
            add_bias(4, 0, SPAN_TILES)
            with pool.Fori(1, spans // 2 - 1) as i:
                for b in range(2):
                    finish(2 * i + b, b, SPAN_TILES, 16 * i)
                    add_bias(2 * i + b + 3, 1 - b, SPAN_TILES)
            finish(spans - 2, 0, SPAN_TILES, 16 * (spans // 2 - 1))

        @block.scalar
        def _(act):
            act.wait_ge(constants, 3)

            def root_batch(j):
                lo, hi = batches[j]
                act.wait_ge(n_stat, 2 * j + 2)
                act.activation(n_dev[:, lo:hi], n_mv[:, lo:hi, 1], ACT.Sqrt, bias=eps[:, 0:1]).then_inc(n_rooted, 1)

            def norm_batch(j):
                act.wait_ge(n_scaled, 2 * j + 2)
                for t in range(batches[j][0], batches[j][1] - by_dve[j]):
                    a = act.activation(xn[:, t, :], x_sb[:, t, :], ACT.Identity, bias=n_shift[:, t:t + 1],
                                       scale=n_rstd[:, t:t + 1])
                a.then_inc(n_act, 1)

            act.activation(spare[:, 0:1], eps[0:1, :], ACT.Sqrt)
            root_batch(0)
            for j in range(1, len(batches)):
                root_batch(j)
                norm_batch(j - 1)
            norm_batch(len(batches) - 1)

            def high_rows(i, s, first):
                if not (first and s < SUM_GAP):
                    act.wait_ge(summed, SLOTS * i + s - SUM_GAP + 1)
                act.wait_ge(gathered[s], 16 * (CHUNKS * i + chunks_of(i, s)))
                if not first:
                    act.sem_inc(passed, 1)
                at = bass.ds(SLOTS * i + s, 1)
                for c in range(chunks_of(i, s)):
                    a = act.activation(x_h[:, s % SUM_BANKS, c, :], raw[:, s, c, :], ACT.Copy,
                                       scale=wgt_t[:, at, c:c + 1].rearrange("p a c -> p (a c)"))
                a.then_inc(x_high, 1)

            def copy_pair(k, n, b):
                if isinstance(k, int) and k >= early:
                    act.wait_ge(projected, k - 1)
                act.copy(agg_pair[:, b, :, 0:n * P], agg_t[:, :, bass.ds(2 * P * k, n * P)]).then_inc(copied, 1)

            def root_pair(k, n, b):
                act.wait_ge(t_stat, 2 * k + 2)
                act.activation(t_dev[:, b, 0:n], t_mv[:, b, 0:n, 1], ACT.Sqrt, bias=eps[:, 0:1]).then_inc(t_rooted, 1)

            def norm_pair(k, n, b):
                act.wait_ge(t_scaled, 2 * k + 2)
                if isinstance(k, int) and k >= early:
                    act.wait_ge(z_turned, k - 1)
                for t in range(n):
                    at = bass.ds(2 * k + t, 1)
                    a = act.activation(z_pair[:, b, t, :], x_sb[:, at, :].rearrange("p a d -> p (a d)"),
                                       ACT.Identity, bias=z_shift[:, at], scale=z_rstd[:, at])
                a.then_inc(z_made, 1)

            def high_pair(k, n, b):
                act.wait_ge(z_turned, k + 1)
                act.copy(zt_h[:, :, bass.ds(2 * P * k, n * P)],
                         ps_turn(k, b)[:, 0:KD * n * P].rearrange("p (k n) -> p k n", k=KD)).then_inc(z_high, 1)

            for c in range(CHUNKS):
                act.wait_ge(turned, TURNED_WGT + c + 1)
                act.copy(wgt_t[:, :, c], ps[(CHUNKS + c) % 3][:, 0:groups]).then_inc(evac_a, 1)
            act.wait_ge(turned, TURNED_DST)
            act.copy(gb[:, :], ps_sum[0][:, 0:2 * dim]).then_inc(spread, 1)
            act.copy(b1_all[:, :, :].rearrange("p e f -> p (e f)"), ps_sum[1][:, 0:experts * FB]).then_inc(spread, 1)
            for c in range(CHUNKS):
                act.wait_ge(turned, TURNED_DST + c + 1)
                act.copy(dst_t[:, :, c], ps[(2 * CHUNKS + c) % 3][:, 0:groups]).then_inc(evac_a, 1)

            def clear_sums():
                act.wait_ge(turned, TURNED_ALL)
                act.activation(agg_t[:, 0, :], zero[:, 0:1].to_broadcast([P, width]), ACT.Copy).then_inc(cleared, 1)
            def root_raw(g):
                act.wait_ge(r_stat, 2 * g + 2)
                act.activation(r_dev[:, g, :], r_mv[:, g, :, 1], ACT.Sqrt, bias=eps[:, 0:1]).then_inc(r_rooted, 1)

            def norm_raw(g):
                act.wait_ge(r_scaled, 2 * g + 2)
                for c in range(CHUNKS):
                    a = act.activation(raw[:, g, c, :], raw[:, g, c, :], ACT.Identity, bias=r_shift[:, g, c:c + 1],
                                       scale=r_rstd[:, g, c:c + 1])
                a.then_inc(r_normed, 1)

            root_raw(0)
            for s in range(SLOTS):
                if s < RAW_GROUPS:
                    norm_raw(s)
                    if s + 1 < RAW_GROUPS:
                        root_raw(s + 1)
                    act.wait_ge(r_normed, s + 1)
                if s == 0:
                    act.wait_ge(evac_a, CHUNKS)
                    act.wait_ge(table_in, 16 * (len(batches) + 1))
                high_rows(0, s, True)
                if s == 1:
                    clear_sums()
            with act.Fori(1, FUSE) as i:
                for s in range(SLOTS):
                    high_rows(i, s, False)
            act.wait_ge(prep, PREP_FLAG)
            flag = act.value_load(regular[0:1, 0:1])
            def act_fused(i, first, last=0):
                for s in range(SLOTS):
                    high_rows(i, s, False)
                    if s == FUSE_SLOT:
                        act.wait_ge(added, SLOTS * i + s - LAG)
                        act.sem_inc(passed, 1)
                        copy_pair(i - FUSE, 2, 0)
                        if not first:
                            high_pair(i - FUSE - 1, 2, 0)
                    if s == 5 + last:
                        root_pair(i - FUSE, 2, 0)
                    if s == 6 + last:
                        norm_pair(i - FUSE, 2, 0)

            def act_late(started):
                q, r = late
                act.wait_ge(added, groups - 1)
                copy_pair(*q)
                if started:
                    norm_pair(early - 1, 2, 0)
                act.wait_ge(added, groups)
                copy_pair(*r)
                for stage, pair in ((root_pair, q), (norm_pair, q), (root_pair, r), (norm_pair, r)):
                    stage(*pair)
                if started:
                    high_pair(early - 1, 2, 0)
                high_pair(*q)
                high_pair(*r)

            with act.If(flag > 0):
                act_fused(FUSE, True)
                with act.Fori(FUSE + 1, rounds - 1) as i:
                    act_fused(i, False)
                act_fused(rounds - 1, False, last=1)
                act_late(True)
            with act.Else():
                with act.Fori(FUSE, rounds - 1) as i:
                    for s in range(SLOTS):
                        high_rows(i, s, False)
                for s in range(SLOTS):
                    high_rows(rounds - 1, s, False)
                act.wait_ge(summed, groups)
                with act.Fori(0, groups) as g:
                    for c in range(CHUNKS):
                        act.wait_ge(gen_mm, windows * CHUNKS * g + windows * c + 1)
                        act.copy(g_idx[:, 0:1], idx_t[:, bass.ds(g, 1), c:c + 1].rearrange("p a c -> p (a c)")
                                 ).then_inc(gen_idx, 1)
                        act.wait_ge(gen_gather, 16 * CHUNKS * g + 16 * c + 16)
                        act.sem_inc(passed, 1)
                        act.activation(x_h[:, 0, 0, :], raw[:, 0, 0, :], ACT.Copy,
                                       scale=wgt_t[:, bass.ds(g, 1), c:c + 1].rearrange("p a c -> p (a c)")
                                       ).then_inc(gen_high, 1)
                act.wait_ge(gen_done, 1)
                with act.Fori(0, early) as k:
                    copy_pair(k, 2, 0)
                    root_pair(k, 2, 0)
                    norm_pair(k, 2, 0)
                    high_pair(k, 2, 0)
                act_late(False)

            act.activation(spare[:, 0:1], eps[0:1, :], ACT.Exp)
            act.wait_ge(route_v, ROUTE_MAX0)
            act.activation(r_exp[:, :], logit[:, :], ACT.Exp, accum_out=r_s[:, 1:2]).then_inc(route_a, 1)
            act.wait_ge(route_v, ROUTE_MAX1)
            act.activation(r_exp[:, :], r_w[:, :], ACT.Exp, accum_out=r_s[:, 3:4]).then_inc(route_a, 1)
            act.wait_ge(route_v, ROUTE_PAIR)
            act.activation(top_w[:, :], r_s[:, 6:8], ACT.Exp, accum_out=r_s[:, 5:6]).then_inc(route_a, 1)
            act.activation(spare[:, 1:2], eps[0:1, :], ACT.Gelu)
            for e in range(2):
                which = act.value_load(top_i[0:1, e:e + 1], min_val=0, max_val=experts - 1)
                act.copy(b1_s[:, e, :], b1_all[:, bass.ds(which, 1), :].rearrange("p a f -> p (a f)")
                         ).then_inc(b1_picked, 1)
            for n in range(2 * HALVES):
                e, at = n // HALVES, slice(n % HALVES * hidden // HALVES, (n % HALVES + 1) * hidden // HALVES)
                act.wait_ge(w1_in[n], 16)
                act.copy(w1_h[:, e, :, at], w1_raw[:, e, :, at]).then_inc(w1_high, 1)
            act.wait_ge(b1_picked, 2)
            act.wait_ge(route_v, ROUTE_BIAS - 2)

            def gelu_span(q, b, cols, free):
                for m in range(HB):
                    n = HB * q + m
                    if m == 0 and free is not None:
                        act.wait_ge(l2_done, free)
                    act.wait_ge(l1_done, n + 1)
                    bias = b1_s[:, m // FB, m % FB:m % FB + 1]
                    act.activation(h_h[:, b, m, 0:cols], ps_hidden[m % 4][:, 0:cols], ACT.Gelu, bias=bias)
                    if not (isinstance(n, int) and n < 2):
                        act.wait_ge(h_low, n - 1)
                    act.activation(h_x[:, m % 2, 0:cols], ps_hidden[m % 4][:, 0:cols], ACT.Gelu,
                                   bias=bias).then_inc(gelu_done, 1)
                    if free is None and q == 0 and m in W2_AFTER:
                        e = W2_AFTER.index(m)
                        act.wait_ge(w2_in[e], 16)
                        act.activation(w2_h[:, e, :, :], w2_raw[:, e, :, :], ACT.Copy,
                                       scale=top_wb[:, e:e + 1]).then_inc(w2_high, 1)

            gelu_span(0, 0, SPAN, None)
            gelu_span(1, 1, SPAN, None)
            with act.Fori(1, spans // 2) as i:
                for b in range(2):
                    gelu_span(2 * i + b, b, SPAN, SPAN_TILES * (2 * i + b - 1))
            gelu_span(spans, 0, P, SPAN_TILES * (spans - 1))
            act.activation(spare[:, 2:3], eps[0:1, :], ACT.Sqrt)
            for n, (b, lo, hi) in enumerate(LAST):
                act.wait_ge(last_stat, 2 * n + 2)
                act.activation(last_dev[:, lo:hi], last_mv[:, lo:hi, 1], ACT.Sqrt,
                               bias=eps[:, 0:1]).then_inc(last_rooted, 1)
                act.wait_ge(last_scaled, 2 * n + 2)
                for j in range(lo, hi):
                    o = o_t[:, b, j - lo, :]
                    a = act.activation(o, o, ACT.Identity, bias=last_shift[:, j:j + 1], scale=last_rstd[:, j:j + 1])
                a.then_inc(last_normed, 1)

        @block.tensor
        def _(pe):
            pe.wait_ge(ident_set, 2)

            def turn_edges(n, rows):
                for m in range(n, n + CHUNKS):
                    if 3 <= m < 7:
                        pe.wait_ge(evac_v, m - 2)
                    elif 7 <= m < 15:
                        pe.wait_ge(evac_a, m - 6)
                    elif m == 15:
                        pe.wait_ge(evac_v, CHUNKS + 1)
                    c = m - n
                    pe.transpose(ps[m % 3][:, 0:groups], rows[0:groups, c * P:c * P + P],
                                 ident[0:groups, 0:groups]).then_inc(turned, 1)

            pe.wait_ge(prep, PREP_SRC)
            turn_edges(0, src_f)
            pe.wait_ge(wgt_in, 48)
            turn_edges(CHUNKS, wgt_rows)
            pe.wait_ge(small_in, 16 * 3)
            pe.wait_ge(constants, 3)
            pe.matmul(ps_sum[0][:, 0:2 * dim], ones[:, :], gb_row[:, :], start=True, stop=True).then_inc(turned, 1)
            pe.transpose(ps_sum[1][:, 0:experts * FB], b1_rows[:, :],
                         ident[0:experts * FB, 0:experts * FB]).then_inc(turned, 1)
            pe.wait_ge(prep, PREP_DST)
            turn_edges(2 * CHUNKS, dst_f)
            pe.wait_ge(prep, PREP_REL)
            turn_edges(3 * CHUNKS, rel_f)
            pe.transpose(ps_r[0:1, 0:groups], g_min[0:groups, :], ident[0:groups, 0:groups]).then_inc(turned, 1)
            pe.transpose(ps_r[0:1, P:P + groups], g_max[0:groups, :], ident[0:groups, 0:groups]).then_inc(turned, 1)
            pe.wait_ge(spread, 2)

            def sum_group(i, s, first):
                g = SLOTS * i + s
                pe.wait_ge(built, g + 1)
                if not (first and s < SUM_GAP):
                    pe.wait_ge(added, g - SUM_GAP + 1)
                pe.wait_ge(x_low, g + 1)
                for k in range(KD):
                    n, chunks = 0, chunks_of(i, s)
                    for part in (x_h, x_l):
                        for c in range(chunks):
                            mm = pe.matmul(ps_sum[s % SUM_BANKS][:, WIN * k:WIN * k + WIN],
                                           part[:, s % SUM_BANKS, c, P * k:P * k + P], onehot[:, s % SUM_BANKS, c, :],
                                           start=(n == 0), stop=(n == 2 * chunks - 1))
                            n += 1
                mm.then_inc(summed, 1)

            def project(k, n, b):
                pe.wait_ge(copied, k + 1)
                if isinstance(k, int) and k >= early:
                    pe.wait_ge(x1_made, k - 1)
                for t in range(n):
                    for h in range(KD):
                        mm = pe.matmul(ps_project[b][:, dim * t:dim * t + dim], agg_pair[:, b, h, P * t:P * t + P],
                                       gw_sb[:, h, :], start=(h == 0), stop=(h == KD - 1))
                mm.then_inc(projected, 1)

            def turn(k, n, b):
                pe.wait_ge(z_made, k + 1)
                if isinstance(k, int) and early <= k < pairs:
                    pe.wait_ge(z_low, k - 1)
                for t in range(n):
                    for h in range(KD):
                        at = P * (n * h + t)
                        mm = pe.transpose(ps_turn(k, b)[:, at:at + P], z_pair[:, b, t, P * h:P * h + P], ident[:, :])
                mm.then_inc(z_turned, 1)

            for s in range(SLOTS):
                sum_group(0, s, True)
            with pe.Fori(1, FUSE) as i:
                for s in range(SLOTS):
                    sum_group(i, s, False)

            def pe_fused(i, first):
                for s in range(SLOTS):
                    sum_group(i, s, False)
                    if s == 0 and not first:
                        turn(i - FUSE - 1, 2, 0)
                    if s == FUSE_SLOT:
                        project(i - FUSE, 2, 0)

            def pe_late(started):
                q, r = late
                project(*q)
                project(*r)
                if started:
                    turn(early - 1, 2, 0)
                turn(*q)
                turn(*r)

            pe.wait_ge(gw_in, 16)
            pe.wait_ge(prep, PREP_FLAG)
            flag = pe.value_load(regular[0:1, 0:1])
            with pe.If(flag > 0):
                pe_fused(FUSE, True)
                with pe.Fori(FUSE + 1, rounds - 1) as i:
                    pe_fused(i, False)
                pe_fused(rounds - 1, False)
                pe_late(True)
            with pe.Else():
                with pe.Fori(FUSE, rounds - 1) as i:
                    for s in range(SLOTS):
                        sum_group(i, s, False)
                for s in range(SLOTS):
                    sum_group(rounds - 1, s, False)
                pe.sem_inc(gen_mm, 1)
                with pe.Fori(0, groups) as g:
                    for c in range(CHUNKS):
                        pe.wait_ge(gen_low, CHUNKS * g + c + 1)
                        pe.sem_inc(passed, 1)
                        with pe.Fori(0, windows) as v:
                            step = windows * CHUNKS * g + windows * c + v
                            pe.wait_ge(gen_hot, step + 1)
                            for k in range(KD):
                                for part in (x_h, x_l):
                                    mm = pe.matmul(ps_sum[0][:, WIN * k:WIN * k + WIN],
                                                   part[:, 0, 0, P * k:P * k + P], onehot[:, 0, 0, :],
                                                   start=(part is x_h), stop=(part is x_l))
                            mm.then_inc(gen_mm, 1)
                with pe.Fori(0, early) as k:
                    project(k, 2, 0)
                    turn(k, 2, 0)
                pe_late(False)

            pe.wait_ge(router_in, 16 * 3)
            pe.wait_ge(route_v, ROUTE_COLS)
            for k in range(KD):
                mm = pe.matmul(ps_r[0:1, 8:8 + experts], col_sum[:, k:k + 1], wr_sb[:, k, :],
                               start=(k == 0), stop=(k == KD - 1))
            mm.then_inc(route_p, 1)
            pe.wait_ge(route_v, ROUTE_DENSE)
            pe.matmul(ps_r[:, 16:18], ones[:, :], top_w[:, :], start=True, stop=True).then_inc(route_p, 1)
            pe.matmul(ps_r[0:experts, P:2 * P], dense[:, 0, :], ones[:, :], start=True, stop=True).then_inc(route_p, 1)
            pe.wait_ge(route_v, ROUTE_DENSE + 2)
            pe.matmul(ps_r[:, 256:256 + dim], dense_b[:, :], b2_sb[:, :], start=True, stop=True).then_inc(route_p, 1)

            def block1(q, m, cols, at, first):
                e, f = m // FB, m % FB
                if first:
                    pe.wait_ge(w1_low, HALVES * m // FB + 1)
                if first and m == 3:
                    pe.wait_ge(route_v, ROUTE_BIAS)
                if not (first and m < 4):
                    pe.wait_ge(gelu_done, HB * q + m - 3)
                n = 0
                for wt, z in ((w1_h, zt_h), (w1_h, zt_l), (w1_l, zt_h)):
                    for k in range(KD):
                        mm = pe.matmul(ps_hidden[m % 4][:, 0:cols], wt[:, e, k, f * P:f * P + P], z[:, k, at],
                                       start=(n == 0), stop=(n == 3 * KD - 1))
                        n += 1
                mm.then_inc(l1_done, 1)

            def tile2(q, b, j, first):
                if first and j == 0:
                    pe.wait_ge(w2_low, 2)
                if j == 0:
                    pe.wait_ge(h_low, HB * q + HB)
                if not (first and j < 2):
                    pe.wait_ge(o_made, SPAN_TILES * q + j - 1)
                n = 0
                for h, wt in ((h_h, w2_h), (h_h, w2_l), (h_l, w2_h)):
                    for m in range(HB):
                        mm = pe.matmul(ps_sum[(SPAN_TILES * b + j) % SUM_BANKS][:, 0:dim],
                                       h[:, b, m, j * P:j * P + P], wt[:, m // FB, m % FB, :],
                                       start=(n == 0), stop=(n == 3 * HB - 1))
                        n += 1
                mm.then_inc(l2_done, 1)

            def layers(q, b, cols, at, first=False):
                for m in range(HB):
                    block1(q, m, cols, at, False)
                    if m in TILE_AFTER:
                        tile2(q - 1, 1 - b, TILE_AFTER.index(m), first)

            for m in range(HB):
                block1(0, m, SPAN, slice(0, SPAN), True)
            layers(1, 1, SPAN, slice(SPAN, 2 * SPAN), first=True)
            with pe.Fori(1, spans // 2) as i:
                for b in range(2):
                    layers(2 * i + b, b, SPAN, bass.ds(2 * SPAN * i + SPAN * b, SPAN))
            layers(spans, 0, P, slice(spans * SPAN, spans * SPAN + P))
            tile2(spans, 0, 0, False)

        @block.vector
        def _(dve):
            dve.memset(src_rows[96:P, :], 0).then_inc(zeroed, 1)
            dve.memset(wgt_rows[96:P, :], 0.0).then_inc(zeroed, 1)
            dve.memset(x_sb[:, tiles - 1:tiles_up, :], 0.0).then_inc(zeroed, 1)
            dve.memset(ones[:, :], 1.0).then_inc(constants, 1)
            dve.memset(eps[:, :], EPS).then_inc(constants, 1)
            dve.memset(zero[:, :], 0.0).then_inc(constants, 1)
            dve.memset(z_rstd[:, :], 0.0)
            dve.memset(z_shift[:, :], 0.0)
            dve.memset(idx_t[:, groups:groups + SLOTS, :], 0)

            dve.wait_ge(src_in, 48)
            dve.tensor_copy(src_f[0:groups, :], src_rows[0:groups, :]).then_inc(prep, 1)
            for c in range(CHUNKS):
                dve.wait_ge(turned, c + 1)
                dve.tensor_copy(idx_t[:, 0:groups, c], ps[c % 3][:, 0:groups]).then_inc(evac_v, 1)
            dve.wait_ge(evac_v, CHUNKS)
            for s in range(SLOTS):
                dve.tensor_copy(idx_slot[:, s, :], idx_t[:, s, :]).then_inc(slot_ready, 1)

            def stat_batch(j):
                lo, hi = batches[j]
                dve.wait_ge(x_in[j], 32 if j == with_tail else 16)
                for t in range(lo, hi):
                    bn = dve.bn_stats(n_stats[:, t, :], x_sb[:, t, :])
                bn.then_inc(n_stat, 1)
                dve.wait_ge(n_stat, 2 * j + 1)
                for t in range(lo, hi):
                    bn = dve.bn_aggr(n_mv[:, t, :], n_stats[:, t, :])
                bn.then_inc(n_stat, 1)

            def scale_batch(j):
                lo, hi = batches[j]
                dve.wait_ge(n_rooted, j + 1)
                dve.reciprocal(n_rstd[:, lo:hi], n_dev[:, lo:hi]).then_inc(n_scaled, 1)
                dve.wait_ge(n_scaled, 2 * j + 1)
                dve.scalar_tensor_tensor(out=n_shift[:, lo:hi], in0=n_mv[:, lo:hi, 0], scalar=-1.0,
                                         in1=n_rstd[:, lo:hi], op0=ALU.mult, op1=ALU.mult).then_inc(n_scaled, 1)
                if by_dve[j]:
                    dve.wait_ge(n_scaled, 2 * j + 2)
                    for t in range(hi - by_dve[j], hi):
                        a = dve.tensor_scalar(xn[:, t, :], x_sb[:, t, :], n_rstd[:, t:t + 1], n_shift[:, t:t + 1],
                                              ALU.mult, ALU.add)
                    a.then_inc(n_dve, 1)

            stat_batch(0)
            for j in range(1, len(batches)):
                stat_batch(j)
                scale_batch(j - 1)
            scale_batch(len(batches) - 1)
            dve.wait_ge(dst_in, 64)
            dve.tensor_copy(dst_f[0:groups, :], dst_rows[0:groups, :]).then_inc(prep, 1)
            dve.wait_ge(prep, 2)
            dve.tensor_reduce(g_min[0:groups, :], dst_f[0:groups, :], AX.X, ALU.min).then_inc(prep, 1)
            dve.tensor_reduce(g_max[0:groups, :], dst_f[0:groups, :], AX.X, ALU.max).then_inc(prep, 1)
            dve.wait_ge(prep, 4)
            dve.tensor_scalar(rel_f[0:groups, :], dst_f[0:groups, :], g_min[0:groups, :], None,
                              ALU.subtract).then_inc(prep, 1)
            dve.wait_ge(counted, 3)
            dve.tensor_copy(iota[:, :], iota_i[:, :]).then_inc(counted, 1)

            def stat_raw(g):
                dve.wait_ge(gathered[g], 16 * CHUNKS)
                for c in range(CHUNKS):
                    bn = dve.bn_stats(r_stats[:, g, c, :], raw[:, g, c, :])
                bn.then_inc(r_stat, 1)
                dve.wait_ge(r_stat, 2 * g + 1)
                for c in range(CHUNKS):
                    bn = dve.bn_aggr(r_mv[:, g, c, :], r_stats[:, g, c, :])
                bn.then_inc(r_stat, 1)

            def scale_raw(g):
                dve.wait_ge(r_rooted, g + 1)
                dve.reciprocal(r_rstd[:, g, :], r_dev[:, g, :]).then_inc(r_scaled, 1)
                dve.wait_ge(r_scaled, 2 * g + 1)
                dve.scalar_tensor_tensor(out=r_shift[:, g, :], in0=r_mv[:, g, :, 0], scalar=-1.0,
                                         in1=r_rstd[:, g, :], op0=ALU.mult, op1=ALU.mult).then_inc(r_scaled, 1)

            stat_raw(0)
            scale_raw(0)
            for c in range(CHUNKS):
                dve.wait_ge(turned, TURNED_REL + c + 1)
                dve.tensor_copy(rel_t[:, :, c], ps[(3 * CHUNKS + c) % 3][:, 0:groups]).then_inc(evac_v, 1)
            dve.wait_ge(turned, TURNED_ALL)
            dve.tensor_copy(base_i[:, 0:groups], ps_r[0:1, 0:groups]).then_inc(prep, 1)
            dve.tensor_copy(base_f[:, 0:groups], ps_r[0:1, 0:groups]).then_inc(prep, 1)
            dve.wait_ge(prep, 7)
            dve.wait_ge(counted, 4)
            dve.wait_ge(evac_v, 2 * CHUNKS)

            def find_regular():
                dve.tensor_copy(first[:, :], first_i[:, :]).then_inc(counted, 1)
                dve.tensor_copy(need_f[:, 0:SLOTS * (early + 1)], need_i[:, 0:SLOTS * (early + 1)]).then_inc(counted, 1)
                dve.wait_ge(counted, 6)
                dve.tensor_tensor(span_row[:, 0:groups], ps_r[0:1, P:P + groups], base_f[:, 0:groups],
                                  ALU.subtract).then_inc(prep, 1)
                checked = groups - first_checked
                dve.tensor_tensor(room_row[:, 0:checked], base_f[:, first_checked:groups], need_f[:, 0:checked],
                                  ALU.subtract).then_inc(prep, 1)
                dve.wait_ge(prep, 9)
                dve.tensor_reduce(worst[:, 0:1], span_row[:, 0:groups], AX.X, ALU.max).then_inc(prep, 1)
                dve.tensor_reduce(worst[:, 1:2], room_row[:, 0:checked], AX.X, ALU.min).then_inc(prep, 1)
                dve.wait_ge(prep, 11)
                dve.tensor_scalar(worst[:, 2:3], worst[:, 0:1], float(WIN), None, ALU.is_lt).then_inc(prep, 1)
                dve.wait_ge(prep, 12)
                dve.tensor_scalar(regular[:, :], worst[:, 1:2], 0.0, worst[:, 2:3], ALU.is_ge,
                                  ALU.mult).then_inc(prep, 1)
                dve.wait_ge(prep, PREP_FLAG)

            def build(i, s, first):
                g = SLOTS * i + s
                if not (first and s < SUM_GAP):
                    dve.wait_ge(summed, g - SUM_GAP + 1)
                dve.tensor_tensor(onehot[:, s % SUM_BANKS, :, :], iota[:, :].unsqueeze(1).to_broadcast([P, CHUNKS, WIN]),
                                  rel_t[:, bass.ds(g, 1), :].rearrange("p a c -> p (a c)").unsqueeze(2).to_broadcast(
                                      [P, CHUNKS, WIN]), ALU.is_equal).then_inc(built, 1)

            def low_rows(i, s):
                g = SLOTS * i + s
                dve.wait_ge(x_high, g + 1)
                at = bass.ds(g, 1)
                for c in range(chunks_of(i, s)):
                    lo = dve.scalar_tensor_tensor(out=x_l[:, s % SUM_BANKS, c, :], in0=raw[:, s, c, :],
                                                  scalar=wgt_t[:, at, c:c + 1].rearrange("p a c -> p (a c)"),
                                                  in1=x_h[:, s % SUM_BANKS, c, :].bitcast(F32), op0=ALU.mult, op1=ALU.subtract)
                lo.then_inc(x_low, 1)

            def stage_indices(i, s):
                g = SLOTS * i + s
                dve.wait_ge(x_low, g + 1)
                dve.sem_inc(passed, 1)
                dve.tensor_copy(idx_slot[:, s, :], idx_t[:, bass.ds(g + SLOTS, 1), :].rearrange("p a c -> p (a c)")
                                ).then_inc(slot_ready, 1)

            def window_of(g):
                return dve.value_load(base_i[0:1, bass.ds(g, 1)], min_val=0, max_val=nodes - 1)

            def add_sums(g, s, base):
                dve.wait_ge(summed, g + 1)
                if not (isinstance(g, int) and g == 0):
                    dve.wait_ge(added, g)
                window = agg_t[:, :, bass.ds(base, WIN)]
                dve.tensor_tensor(window, window,
                                  ps_sum[s % SUM_BANKS][:, 0:KD * WIN].rearrange("p (k w) -> p k w", k=KD),
                                  ALU.add).then_inc(added, 1)

            def make_x1(k, n, b):
                at = x_sb[:, bass.ds(2 * k, n), :]
                dve.wait_ge(projected, k + 1)
                dve.tensor_tensor(at, at, ps_project[b][:, 0:n * dim].rearrange("p (t d) -> p t d", t=n),
                                  ALU.add).then_inc(x1_made, 1)
                dve.wait_ge(x1_made, k + 1)
                dve.sem_inc(passed, 1)
                for t in range(n):
                    bn = dve.bn_stats(t_stats[:, b, t, :],
                                      x_sb[:, bass.ds(2 * k + t, 1), :].rearrange("p a d -> p (a d)"))
                bn.then_inc(t_stat, 1)
                dve.wait_ge(t_stat, 2 * k + 1)
                dve.sem_inc(passed, 1)
                for t in range(n):
                    bn = dve.bn_aggr(t_mv[:, b, t, :], t_stats[:, b, t, :])
                bn.then_inc(t_stat, 1)

            def scale_pair(k, n, b):
                at = bass.ds(2 * k, n)
                dve.wait_ge(t_rooted, k + 1)
                dve.reciprocal(z_rstd[:, at], t_dev[:, b, 0:n]).then_inc(t_scaled, 1)
                dve.wait_ge(t_scaled, 2 * k + 1)
                dve.scalar_tensor_tensor(out=z_shift[:, at], in0=t_mv[:, b, 0:n, 0], scalar=-1.0,
                                         in1=z_rstd[:, at], op0=ALU.mult, op1=ALU.mult).then_inc(t_scaled, 1)

            def turned_z(k, n, b):
                return ps_turn(k, b)[:, 0:KD * n * P].rearrange("p (k n) -> p k n", k=KD)

            def count_pair(k, n, b):
                dve.wait_ge(z_high, k + 1)
                real = n * P if n == 2 else tail
                dve.tensor_reduce(z_sums[:, :, bass.ds(k, 1)].rearrange("p k a -> p (k a)"),
                                  turned_z(k, n, b)[:, :, 0:real], AX.X, ALU.add).then_inc(z_counted, 1)

            def low_pair(k, n, b):
                dve.wait_ge(z_high, k + 1)
                at = bass.ds(2 * P * k, n * P)
                dve.tensor_tensor(zt_l[:, :, at], turned_z(k, n, b), zt_h[:, :, at].bitcast(F32),
                                  ALU.subtract).then_inc(z_low, 1)

            for s in range(SLOTS):
                build(0, s, True)
                if s + 1 < RAW_GROUPS:
                    stat_raw(s + 1)
                    scale_raw(s + 1)
                if s == LAG:
                    dve.wait_ge(cleared, 2)
                low_rows(0, s)
                stage_indices(0, s)
                if s >= LAG:
                    add_sums(s - LAG, s - LAG, window_of(s - LAG))
            find_regular()

            def dve_step(i, s, base):
                g = SLOTS * i + s - LAG
                build(i, s, False)
                add_sums(g, (s - LAG) % SLOTS, base)
                low_rows(i, s)
                following = window_of(g + 1)
                stage_indices(i, s)
                return following

            def dve_round(i):
                base = window_of(SLOTS * i - LAG)
                for s in range(SLOTS):
                    base = dve_step(i, s, base)

            def last_sums(started):
                for g, base in zip(range(groups - LAG, groups), last_bases):
                    if started and g == groups - 1:
                        scale_pair(early - 1, 2, 0)
                    add_sums(g, g % SLOTS, base)

            def dve_late(started):
                q, r = late
                make_x1(*q)
                scale_pair(*q)
                make_x1(*r)
                scale_pair(*r)
                if started:
                    count_pair(early - 1, 2, 0)
                    low_pair(early - 1, 2, 0)
                count_pair(*q)
                count_pair(*r)

            with dve.Fori(1, FUSE) as i:
                dve_round(i)
            flag = dve.value_load(regular[0:1, 0:1])
            last_bases = [window_of(g) for g in range(groups - LAG, groups)]

            def dve_fused(i, first, last=False):
                base = window_of(SLOTS * i - LAG)
                for s in range(SLOTS):
                    base = dve_step(i, s, base)
                    if s == 3 and not first:
                        count_pair(i - FUSE - 1, 2, 0)
                        low_pair(i - FUSE - 1, 2, 0)
                    if s == (6 if last else 4):
                        make_x1(i - FUSE, 2, 0)
                    if s == 5 and not last:
                        scale_pair(i - FUSE, 2, 0)

            with dve.If(flag > 0):
                dve_fused(FUSE, True)
                with dve.Fori(FUSE + 1, rounds - 1) as i:
                    dve_fused(i, False)
                dve_fused(rounds - 1, False, last=True)
                last_sums(True)
                dve_late(True)
            with dve.Else():
                with dve.Fori(FUSE, rounds - 1) as i:
                    dve_round(i)
                dve_round(rounds - 1)
                last_sums(False)
                with dve.Fori(0, groups) as g:
                    gat = bass.ds(g, 1)
                    rel_g = rel_t[:, gat, :].rearrange("p a c -> p (a c)")
                    dst_g = dst_t[:, gat, :].rearrange("p a c -> p (a c)")
                    dve.tensor_scalar(g_key[:, :], rel_g, float(WIN), None, ALU.is_ge).then_inc(gen_key, 1)
                    dve.wait_ge(gen_key, 3 * g + 1)
                    dve.scalar_tensor_tensor(out=g_key[:, :], in0=dst_g, scalar=1.0, in1=g_key[:, :],
                                             op0=ALU.add, op1=ALU.mult).then_inc(gen_key, 1)
                    dve.wait_ge(gen_key, 3 * g + 2)
                    dve.tensor_scalar(g_key[:, :], g_key[:, :], -1.0, None, ALU.add).then_inc(gen_key, 1)
                    dve.wait_ge(gen_key, 3 * g + 3)
                    for c in range(CHUNKS):
                        done = CHUNKS * g + c
                        dve.wait_ge(gen_high, done + 1)
                        dve.sem_inc(passed, 1)
                        dve.scalar_tensor_tensor(out=x_l[:, 0, 0, :], in0=raw[:, 0, 0, :],
                                                 scalar=wgt_t[:, gat, c:c + 1].rearrange("p a c -> p (a c)"),
                                                 in1=x_h[:, 0, 0, :].bitcast(F32), op0=ALU.mult,
                                                 op1=ALU.subtract).then_inc(gen_low, 1)
                        with dve.Fori(0, windows) as v:
                            step = windows * done + v
                            dve.tensor_scalar(g_hit[:, 0:1], g_key[:, c:c + 1], first[:, bass.ds(v, 1)], None,
                                              ALU.subtract).then_inc(gen_win, 1)
                            dve.wait_ge(gen_win, step + 1)
                            dve.tensor_scalar(onehot[:, 0, 0, :], iota[:, :], g_hit[:, 0:1], None,
                                              ALU.is_equal).then_inc(gen_hot, 1)
                            dve.wait_ge(gen_mm, step + 2)
                            window = agg_t[:, :, bass.ds(WIN * v, WIN)]
                            dve.tensor_tensor(window, window,
                                              ps_sum[0][:, 0:KD * WIN].rearrange("p (k w) -> p k w", k=KD),
                                              ALU.add).then_inc(gen_add, 1)
                            dve.wait_ge(gen_add, step + 1)
                dve.sem_inc(gen_done, 1)
                with dve.Fori(0, early) as k:
                    make_x1(k, 2, 0)
                    scale_pair(k, 2, 0)
                    count_pair(k, 2, 0)
                    low_pair(k, 2, 0)
                dve_late(False)

            def make_res(q, b):
                if not (isinstance(q, int) and q < 2):
                    dve.wait_ge(o_made, SPAN_TILES * (q - 1))
                    dve.sem_inc(passed, 1)
                for t in range(SPAN_TILES):
                    at = bass.ds(SPAN_TILES * q + t, 1)
                    r = dve.tensor_scalar(res[:, b, t, :], x_sb[:, at, :].rearrange("p a d -> p (a d)"),
                                          z_rstd[:, at], z_shift[:, at], ALU.mult, ALU.add)
                r.then_inc(res_made, 1)

            def low_w1(n):
                e, at = n // HALVES, slice(n % HALVES * hidden // HALVES, (n % HALVES + 1) * hidden // HALVES)
                dve.wait_ge(w1_high, n + 1)
                dve.tensor_tensor(w1_l[:, e, :, at], w1_raw[:, e, :, at], w1_h[:, e, :, at].bitcast(F32),
                                  ALU.subtract).then_inc(w1_low, 1)

            count = [0]

            def step(ins):
                count[0] += 1
                ins.then_inc(route_v, 1)
                dve.wait_ge(route_v, count[0])

            dve.wait_ge(z_counted, pairs + 1)
            step(dve.tensor_reduce(col_sum[:, :], z_sums[:, :, :], AX.X, ALU.add))
            assert count[0] == ROUTE_COLS
            low_pair(*late[0])
            dve.wait_ge(route_p, 1)
            step(dve.scalar_tensor_tensor(out=logit[:, :], in0=ps_r[0:1, 8:8 + experts], scalar=1.0 / nodes,
                                          in1=br_sb[:, :], op0=ALU.mult, op1=ALU.add))
            step(dve.tensor_reduce(r_s[:, 0:1], logit[:, :], AX.X, ALU.max))
            step(dve.tensor_scalar(logit[:, :], logit[:, :], r_s[:, 0:1], None, ALU.subtract))
            assert count[0] == ROUTE_MAX0
            low_pair(*late[1])
            dve.wait_ge(route_a, 1)
            step(dve.reciprocal(r_s[:, 1:2], r_s[:, 1:2]))
            dve.tensor_scalar(r_w[:, :], r_exp[:, :], r_s[:, 1:2], None, ALU.mult)
            step(dve.tensor_scalar(r_scale[:, :], r_exp[:, :], r_s[:, 1:2], float(nodes), ALU.mult, ALU.mult))
            step(dve.reciprocal(r_scale[:, :], r_scale[:, :]))
            step(dve.tensor_scalar(r_scale[:, :], r_scale[:, :], capacity, 1.0, ALU.mult, ALU.min))
            step(dve.tensor_tensor(r_w[:, :], r_w[:, :], r_scale[:, :], ALU.mult))
            step(dve.tensor_reduce(r_s[:, 2:3], r_w[:, :], AX.X, ALU.max))
            step(dve.tensor_scalar(r_w[:, :], r_w[:, :], r_s[:, 2:3], None, ALU.subtract))
            assert count[0] == ROUTE_MAX1
            dve.wait_ge(route_a, 2)
            step(dve.reciprocal(r_s[:, 3:4], r_s[:, 3:4]))
            step(dve.tensor_scalar(r_w[:, :], r_exp[:, :], r_s[:, 3:4], None, ALU.mult))
            step(dve.max(top_v[:, :], r_w[:, :]))
            step(dve.max_index(top_i[:, :], top_v[:, :], r_w[:, :]))
            assert count[0] == ROUTE_TOP
            step(dve.tensor_scalar(r_s[:, 6:8], top_v[:, 0:2], top_v[:, 0:1], None, ALU.subtract))
            assert count[0] == ROUTE_PAIR
            step(dve.tensor_copy(top_if[:, :], top_i[:, :]))
            dve.wait_ge(route_a, 3)
            step(dve.reciprocal(r_s[:, 5:6], r_s[:, 5:6]))
            step(dve.tensor_scalar(top_w[:, :], top_w[:, :], r_s[:, 5:6], None, ALU.mult))
            for e in range(2):
                step(dve.tensor_scalar(dense[:, e, :], iota[0:1, 0:experts], top_if[:, e:e + 1], top_w[:, e:e + 1],
                                       ALU.is_equal, ALU.mult))
            step(dve.tensor_tensor(dense[:, 0, :], dense[:, 0, :], dense[:, 1, :], ALU.add))
            assert count[0] == ROUTE_DENSE
            make_res(0, 0)
            dve.wait_ge(route_p, 3)
            step(dve.tensor_copy(top_wb[:, :], ps_r[:, 16:18]))
            step(dve.tensor_copy(dense_b[:, :], ps_r[0:experts, P:2 * P]))
            make_res(1, 1)
            low_w1(0)
            dve.wait_ge(route_p, 4)
            step(dve.tensor_copy(bias_b[:, :], ps_r[:, 256:256 + dim]))
            assert count[0] == ROUTE_BIAS

            def low_block(q, b, m, cols):
                dve.wait_ge(gelu_done, HB * q + m + 1)
                dve.tensor_tensor(h_l[:, b, m, 0:cols], h_x[:, m % 2, 0:cols], h_h[:, b, m, 0:cols].bitcast(F32),
                                  ALU.subtract).then_inc(h_low, 1)

            def sum_tile(q, b, j, reused=True):
                if j == 0:
                    dve.wait_ge(res_biased, q + 1)
                    if reused:
                        dve.wait_ge(y_gamma, q)
                dve.wait_ge(l2_done, SPAN_TILES * q + j + 1)
                dve.tensor_tensor(o_t[:, b, j, :], res[:, b, j, :],
                                  ps_sum[(SPAN_TILES * b + j) % SUM_BANKS][:, 0:dim], ALU.add).then_inc(o_made, 1)

            def newton(q, k, ins):
                ins.then_inc(root, 1)
                dve.wait_ge(root, NEWTON_STEPS * q + k + 1)

            def norm_part(q, b, n, part):
                v, y, e = f_var[:, 0:n], f_root[:, 0:n], f_corr[:, 0:n]
                if part == 0:
                    dve.wait_ge(o_made, SPAN_TILES * q + n)
                    dve.sem_inc(passed, 1)
                    for j in range(n):
                        bn = dve.bn_stats(f_stats[:, j, :], o_t[:, b, j, :])
                    bn.then_inc(o_stat, 1)
                if part == 1:
                    dve.wait_ge(o_stat, 2 * q + 1)
                    dve.sem_inc(passed, 1)
                    for j in range(n):
                        bn = dve.bn_aggr(f_mv[:, j, :], f_stats[:, j, :])
                    bn.then_inc(o_stat, 1)
                if part == 2:
                    dve.wait_ge(o_stat, 2 * q + 2)
                    newton(q, 0, dve.tensor_scalar(v, f_mv[:, 0:n, 1], EPS, None, ALU.add))
                    newton(q, 1, dve.tensor_scalar(y.bitcast(I32), v.bitcast(I32), 1, None, ALU.logical_shift_right))
                    newton(q, 2, dve.tensor_scalar(y.bitcast(I32), y.bitcast(I32), -1.0, ROOT_MAGIC,
                                                   ALU.mult, ALU.add))
                if 3 <= part < 3 + NEWTON:
                    k = 3 + 4 * (part - 3)
                    newton(q, k, dve.tensor_tensor(e, y, y, ALU.mult))
                    newton(q, k + 1, dve.tensor_tensor(e, e, v, ALU.mult))
                    newton(q, k + 2, dve.tensor_scalar(e, e, -0.5, 1.5, ALU.mult, ALU.add))
                    newton(q, k + 3, dve.tensor_tensor(y, y, e, ALU.mult))
                if part == 6:
                    dve.scalar_tensor_tensor(out=f_shift[:, 0:n], in0=f_mv[:, 0:n, 0], scalar=-1.0, in1=y,
                                             op0=ALU.mult, op1=ALU.mult).then_inc(f_shifted, 1)
                if part == 7:
                    dve.wait_ge(f_shifted, q + 1)
                    for j in range(n):
                        o = dve.tensor_scalar(o_t[:, b, j, :], o_t[:, b, j, :], f_root[:, j:j + 1],
                                              f_shift[:, j:j + 1], ALU.mult, ALU.add)
                    o.then_inc(o_normed, 1)

            for n in range(1, 2 * HALVES):
                low_w1(n)
            for m in range(HB):
                low_block(0, 0, m, SPAN)
                if m in W2_AFTER:
                    e = W2_AFTER.index(m)
                    dve.wait_ge(w2_high, e + 1)
                    dve.scalar_tensor_tensor(out=w2_l[:, e, :, :], in0=w2_raw[:, e, :, :],
                                             scalar=top_wb[:, e:e + 1], in1=w2_h[:, e, :, :].bitcast(F32),
                                             op0=ALU.mult, op1=ALU.subtract).then_inc(w2_low, 1)
            for m in range(HB):
                low_block(1, 1, m, SPAN)
                if m in SUM_AFTER:
                    sum_tile(0, 0, SUM_AFTER.index(m), reused=False)
            make_res(2, 0)
            with dve.Fori(1, spans // 2) as i:
                for b in (1, 0):
                    q = 2 * i - b
                    for m in range(HB):
                        low_block(q + 1, 1 - b, m, SPAN)
                        norm_part(q - 1, 1 - b, SPAN_TILES, m)
                        if m in SUM_AFTER:
                            sum_tile(q, b, SUM_AFTER.index(m))
                    make_res(q + 2, b)
            for m in range(HB):
                low_block(spans, 0, m, P)
                norm_part(spans - 2, 0, SPAN_TILES, m)
                if m in SUM_AFTER:
                    sum_tile(spans - 1, 1, SUM_AFTER.index(m))

            def stat_last(n):
                b, lo, hi = LAST[n]
                dve.wait_ge(o_made, tiles - SPAN_TILES - 1 + hi)
                for j in range(lo, hi):
                    bn = dve.bn_stats(last_stats[:, j, :], o_t[:, b, j - lo, :])
                bn.then_inc(last_stat, 1)
                dve.wait_ge(last_stat, 2 * n + 1)
                for j in range(lo, hi):
                    bn = dve.bn_aggr(last_mv[:, j, :], last_stats[:, j, :])
                bn.then_inc(last_stat, 1)

            def scale_last(n):
                b, lo, hi = LAST[n]
                dve.wait_ge(last_rooted, n + 1)
                dve.reciprocal(last_rstd[:, lo:hi], last_dev[:, lo:hi]).then_inc(last_scaled, 1)
                dve.wait_ge(last_scaled, 2 * n + 1)
                dve.scalar_tensor_tensor(out=last_shift[:, lo:hi], in0=last_mv[:, lo:hi, 0], scalar=-1.0,
                                         in1=last_rstd[:, lo:hi], op0=ALU.mult, op1=ALU.mult).then_inc(last_scaled, 1)

            def gamma_last(n, y):
                b, lo, hi = LAST[n]
                dve.wait_ge(last_normed, n + 1)
                dve.tensor_tensor(y, o_t[:, b, 0:hi - lo, :],
                                  gb[:, 0:dim].unsqueeze(1).to_broadcast([P, hi - lo, dim]),
                                  ALU.mult).then_inc(last_gamma, 1)

            def x1_last(n, y):
                b, lo, hi = LAST[n]
                dve.wait_ge(last_gamma, n + 1)
                dve.tensor_tensor(y, y, x_sb[:, tiles - SPAN_TILES - 1 + lo:tiles - SPAN_TILES - 1 + hi, :],
                                  ALU.add).then_inc(last_made, 1)

            y_a, y_z = y_out[:, 1, :, :], y_last[:, :].unsqueeze(1)
            stat_last(0)
            scale_last(0)
            sum_tile(spans, 0, 0)
            stat_last(1)
            dve.wait_ge(stored[1], 16 * (spans // 2 - 1))
            dve.wait_ge(x1_beta, spans + 1)
            gamma_last(0, y_a)
            scale_last(1)
            x1_last(0, y_a)
            gamma_last(1, y_z)
            x1_last(1, y_z)


_INS = ["x", "src", "dst", "edge_weight", "L0_gnn_weight", "L0_ffn_Wr", "L0_ffn_br", "L0_ffn_W1", "L0_ffn_b1",
        "L0_ffn_W2", "L0_ffn_b2", "L0_ffn_gamma", "L0_ffn_beta"]


def kernel(**inputs):
    import numpy as _np
    import concourse.bacc as _bacc
    from concourse import mybir as _mybir
    from concourse.bass_utils import run_bass_kernel_spmd as _run

    nc = _bacc.Bacc("TRN2", target_bir_lowering=False, num_devices=1)
    arrays, args = {}, []
    for name in _INS:
        a = _np.ascontiguousarray(inputs[name])
        arrays[f"in_{name}_dram"] = a
        args.append(nc.dram_tensor(f"in_{name}_dram", a.shape, _mybir.dt.from_np(a.dtype), kind="ExternalInput").ap())
    out = nc.dram_tensor("out_0_dram", inputs["x"].shape, _mybir.dt.float32, kind="ExternalOutput").ap()
    table = nc.dram_tensor("table", inputs["x"].shape, _mybir.dt.float32).ap()
    gnn_moe(nc, *args, table, out)
    r = _run(nc, [arrays], core_ids=[0])
    return r.results[0]["out_0_dram"]
```
